# Optimizing a Trainium2 kernel written in Bass

```python
import numpy as np
import jax
import jax.numpy as jnp

def _softmax(x, axis=-1):
    return jax.nn.softmax(x, axis=axis)

def _gelu(x):
    return jax.nn.gelu(x, approximate=True)

def _silu(x):
    return jax.nn.silu(x)

def _sigmoid(x):
    return jax.nn.sigmoid(x)

def _layernorm(x, axis=-1, eps=1e-05):
    m = jnp.mean(x, axis=axis, keepdims=True)
    v = jnp.var(x, axis=axis, keepdims=True)
    return (x - m) / jnp.sqrt(v + eps)

def _scatter_add(tgt, idx, src, axis=0):
    return tgt.at[idx].add(src)

def _segment_sum(src, seg, n):
    return jax.ops.segment_sum(src, seg, n)
kernel_name = 'mk_adj_resnorm_d2_adj_r2_572d19'

def setup_inputs(seed: int=0):
    np.random.seed(seed)
    _w = jnp.asarray

    def _rec_inputs():
        import jax
        import jax.numpy as jnp
        _gk = jax.random.key(seed)
        x = -0.0002928 + 1 * jax.random.normal(jax.random.fold_in(_gk, 1), (8192, 128), jnp.float32)
        _a = jax.random.bernoulli(jax.random.fold_in(_gk, 2), 0.00195312, (8192, 8192))
        _a = jnp.logical_or(_a, jnp.swapaxes(_a, -1, -2))
        _a = jnp.logical_or(_a, jnp.eye(8192, dtype=bool))
        adj = _a.astype(jnp.int32)
        return (x, adj)
    x, adj = _rec_inputs()

    def _L0_gnn_setup():
        import jax, jax.numpy as jnp
        import numpy as np
        N = 8192
        F_IN = 128
        F_OUT = 128
        key = jax.random.key(seed)
        k1, k2, k3 = jax.random.split(key, 3)
        x = jax.random.normal(k1, (N, F_IN), dtype=jnp.float32)
        adj = jax.random.randint(k2, (N, N), 0, 2, dtype=jnp.int32)
        stdv = np.sqrt(6.0 / (2 * F_IN + F_OUT)).astype(np.float32)
        weight = jax.random.uniform(k3, (2 * F_IN, F_OUT), dtype=jnp.float32, minval=-stdv, maxval=stdv)
        bias = jnp.zeros((F_OUT,), dtype=jnp.float32)
        return {'x': x, 'adj': adj, 'weight': weight, 'bias': bias}
    _L0_gnn_all = _L0_gnn_setup()
    _L0_gnn_in = {k: v for k, v in _L0_gnn_all.items() if k in ('weight', 'bias')}
    del _L0_gnn_all

    def _L1_gnn_setup():
        import jax, jax.numpy as jnp
        import numpy as np
        N, IN_DIM, OUT_DIM = (4096, 128, 128)
        key = jax.random.key(seed)
        k1, k2, k3, k4 = jax.random.split(key, 4)
        x = jax.random.normal(k1, (N, IN_DIM), dtype=jnp.float32)
        adj = jax.random.randint(k2, (N, N), 0, 2, dtype=jnp.int32)
        W = jax.random.normal(k3, (OUT_DIM, IN_DIM), dtype=jnp.float32) / np.sqrt(IN_DIM)
        a = jax.random.normal(k4, (2 * OUT_DIM,), dtype=jnp.float32) / np.sqrt(2 * OUT_DIM)
        return {'x': x, 'adj': adj, 'W': W, 'a': a}
    _L1_gnn_all = _L1_gnn_setup()
    _L1_gnn_in = {k: v for k, v in _L1_gnn_all.items() if k in ('W', 'a')}
    del _L1_gnn_all
    return {'x': x, 'adj': adj, 'L0_gnn_weight': _L0_gnn_in['weight'], 'L0_gnn_bias': _L0_gnn_in['bias'], 'L1_gnn_W': _L1_gnn_in['W'], 'L1_gnn_a': _L1_gnn_in['a']}

def reference(x, adj, L0_gnn_weight, L0_gnn_bias, L1_gnn_W, L1_gnn_a):
    import jax
    import jax.numpy as jnp

    def _L0_gnn_ref(x, adj, weight, bias):
        import jax, jax.numpy as jnp
        import numpy as np
        N = 8192
        F_IN = 128
        F_OUT = 128
        a = adj.astype(x.dtype)
        deg = jnp.sum(a, axis=1, keepdims=True)
        x1 = a @ x / deg
        n_x = jnp.concatenate([x1, x], axis=1)
        return n_x @ weight + bias

    def _L1_gnn_ref(x, adj, W, a):
        import jax, jax.numpy as jnp
        import numpy as np
        N, IN_DIM, OUT_DIM = (4096, 128, 128)
        h = jnp.einsum('ni,oi->no', x, W)
        out_dim = W.shape[0]
        a1, a2 = (a[:out_dim], a[out_dim:])
        e_i = h @ a1
        e_j = h @ a2
        e = e_i[:, None] + e_j[None, :]
        e = jnp.where(adj == 0, -jnp.inf, e)
        attn_weights = jax.nn.softmax(e, axis=1)
        h_new = attn_weights @ h
        return h_new
    x = _layernorm(x + _L0_gnn_ref(x, adj, L0_gnn_weight, L0_gnn_bias), axis=-1)
    x = _layernorm(x + _L1_gnn_ref(x, adj, L1_gnn_W, L1_gnn_a), axis=-1)
    return x

_drawn_inputs = setup_inputs


def setup_inputs(seed=0):
    import zlib

    import numpy as np

    out = dict(_drawn_inputs(seed))
    spreads = {'L0_gnn_bias': (0.0, 0.1)}
    factors = {}
    for name, (base, spread) in spreads.items():
        noise = np.random.default_rng([zlib.crc32(name.encode()), seed]).standard_normal(out[name].shape)
        drawn = base * np.exp(spread * noise) if base else spread * noise
        out[name] = jnp.asarray(drawn.astype(out[name].dtype))
    for name, factor in factors.items():
        out[name] = (out[name] * factor).astype(out[name].dtype)
    return out
```

```python
import math
from contextlib import ExitStack

import concourse.bass as bass
from concourse import mybir


def bass_two_graph_layers(
    nc: bass.Bass,
    x: bass.AP,
    adj: bass.AP,
    w0: bass.AP,
    b0: bass.AP,
    w1: bass.AP,
    a1: bass.AP,
    out: bass.AP,
):
    fp32, fp16, fp8 = mybir.dt.float32, mybir.dt.float16, mybir.dt.float8e4
    i32, u32 = mybir.dt.int32, mybir.dt.uint32
    ALU, ACT, AX = mybir.AluOpType, mybir.ActivationFunctionType, mybir.AxisListType

    N, F = x.shape
    P = 128
    QUAD = 32
    NQ = P // QUAD
    JQ = N // NQ
    BYTES = 4
    NB = JQ // (QUAD * BYTES)
    NBLK = NB * BYTES
    TILES = N // P
    GROUP = 4
    GROUPS = TILES // GROUP
    TW = NB * P
    SLOTS = 4
    QS = 8
    HCOLS = F + 1
    XCOLS = 2 * F + 2
    LO = F + 1
    COUNT = F

    XSCALE = 4096.0
    X_MAX, X_MIN = 15.0, 2.0 ** -14
    E_SPAN = 9.0
    W_SHIFT = 11.0 * math.log(2.0)
    W_NORM2 = 7.0
    EPS = 1e-5
    EDGE = [0x38, 0x38, 0x38, 0x40]
    BIT = [0x08, 0x10, 0x20, 0x40]

    def every_byte(b):
        return b * 0x01010101

    packed_dram = nc.dram_tensor("packed_adj", (GROUPS, P, TW), u32, kind="Internal").ap()
    h_dram = nc.dram_tensor("h_rows", (N, HCOLS), fp32, kind="Internal").ap()
    e_dram = nc.dram_tensor("e_row", (TILES, P), fp32, kind="Internal").ap()

    x_quarters = x.rearrange("(a b p c) f -> a p b (c f)", a=NQ, b=NB, c=BYTES)
    h_quarters = h_dram.rearrange("(a b p c) f -> a p b (c f)", a=NQ, b=NB, c=BYTES)
    adj_halves = adj.rearrange("(n g q) (a j) -> n a q g j", g=2, q=QUAD, a=NQ)
    x_tiles = x.rearrange("(t p) f -> t p f", p=P)
    h_tiles = h_dram.rearrange("(t p) f -> t p f", p=P)
    adj_tiles = adj.rearrange("(t p) j -> t p j", p=P)
    e_tiles = e_dram.rearrange("t (p o) -> t p o", o=1)
    e_halves = e_dram.rearrange("(s o t) p -> s o (t p)", s=2, o=1)
    out_tiles = out.rearrange("(t p) f -> t p f", p=P)

    ctx = ExitStack()
    with ctx:
        def sb(name, shape, dt):
            return ctx.enter_context(nc.sbuf_tensor(name, shape, dt))

        def ps(name):
            return ctx.enter_context(nc.psum_tensor(name, [P, 512], fp32))

        def sem(name):
            return ctx.enter_context(nc.semaphore(name))

        adj_in = sb("adj_in", [P, SLOTS, 2, JQ], i32)
        edges = sb("edges", [P, 2, GROUP, JQ], fp8)
        edgesT = sb("edgesT", [P, 2, TW], u32)
        packed = sb("packed", [P, TW], u32)
        parts = sb("parts", [P, NBLK, XCOLS], fp16)
        x1 = sb("x1", [P, TILES, F], fp32)
        x1_row = sb("x1_row", [P, 2, F], fp32)
        x_stage = x1[:, :, :]
        adj_flat = adj_in[:, :, :, :].rearrange("p s g j -> p (s g j)")
        packed_in = adj_flat[:, 0:2 * TW].bitcast(u32).rearrange("p (s w) -> p s w", s=2)
        stage = adj_flat[:, 2 * TW:2 * TW + NBLK * HCOLS].bitcast(fp32).rearrange("p (n f) -> p n f", f=HCOLS)
        stray = sb("stray", [P, TW], u32)
        x_row = sb("x_row", [P, 2, F], fp32)
        xb = sb("xb", [P, 2, F], fp32)
        agg_lo = sb("agg_lo", [P, F + 1], fp32)
        agg = sb("agg", [P, 2, F], fp32)
        catT = sb("catT", [P, 2, 2 * P], fp32)
        z = sb("z", [P, F], fp32)
        zsum = sb("zsum", [P, F + 1], fp32)
        stats = sb("stats", [P, 6], fp32)
        mean_var = sb("mean_var", [P, 2], fp32)
        std = sb("std", [P, 1], fp32)
        rstd = sb("rstd", [P, 1], fp32)
        rcount = sb("rcount", [P, 1], fp32)
        x1T = sb("x1T", [P, 2, P], fp32)
        h_row = sb("h_row", [P, 2, HCOLS], fp32)
        e_all = sb("e_all", [P, TILES], fp32)
        y_out = sb("y_out", [P, 2, F], fp32)
        w0_sb = sb("w0_sb", [P, 2, F], fp32)
        w1_sb = sb("w1_sb", [P, F], fp32)
        w1T = sb("w1T", [P, HCOLS], fp32)
        a2_sb = sb("a2_sb", [P, 1], fp32)
        bias = sb("bias", [P, F], fp32)
        ident = sb("ident", [P, P], fp32)
        ones = sb("ones", [1, P], fp32)
        eps = sb("eps", [P, 1], fp32)
        x_big = sb("x_big", [P, NBLK], fp32)
        w_sq = sb("w_sq", [P, F], fp32)
        gate = sb("gate", [P, 8], fp32)
        okay = sb("okay", [P, 4], fp32)
        top_row = sb("top_row", [P, 1], fp32)
        top = sb("top", [1, 3], fp32)
        verdict = sb("verdict", [1, 4], fp32)
        flag = sb("flag", [1, 1], i32)
        shift = sb("shift", [P, 1], fp32)

        g_adj = adj_flat[:, 0:N]
        g_rows = adj_flat[:, N:2 * N].bitcast(fp32)
        g_mat = parts[:, :, :].rearrange("p n f -> p (n f)").bitcast(fp32).rearrange("p (n f) -> p n f", f=HCOLS)
        g_e = [buf[:, :, :].rearrange("p a b -> p (a b)") for buf in (edges[:, :, :, :].rearrange("p s g j -> p s (g j)"), edgesT)]
        g_e = [half.bitcast(fp32) for half in g_e]
        g_blockT = sb("g_blockT", [P, 2, 4 * P], fp32)

        ps_agg = [ps("ps_agg0"), ps("ps_agg1")]
        ps_catT = ps("ps_catT")
        ps_y = ps("ps_y")
        ps_x1T = ps("ps_x1T")
        ps_h = ps("ps_h")
        ps_small = ps("ps_small")
        g_banks = [ps_agg[1], ps_small]

        s_xload = sem("x_landed")
        s_const = sem("weights_landed")
        s_fill = sem("constants_filled")
        s_stray0 = sem("stray_cleared")
        s_id = sem("ident_cleared")
        s_w1T = sem("w1T_done")
        s_w1Tc = sem("w1T_copied")
        s_hi0 = sem("x_hi_made")
        s_lo0 = sem("x_lo_made")
        s_gate0 = sem("gates0_made")
        s_adj = [sem(f"adj_landed{s}") for s in range(SLOTS)]
        s_conv = sem("converted")
        s_tr = sem("transposed")
        s_check = sem("checked")
        s_pack = sem("tile_packed")
        s_pkst = sem("packed_stored")
        s_agg = sem("agg_summed")
        s_rdeg = sem("rdegree_made")
        s_aglo = sem("agg_lo_scaled")
        s_aggr = sem("agg_made")
        s_xrow = [sem(f"x_row_landed{s}") for s in range(2)]
        s_xb = sem("x_plus_bias_made")
        s_catT = sem("catT_done")
        s_catTc = sem("catT_copied")
        s_y = sem("y_done")
        s_z = sem("z_made")
        s_bn = sem("bn_made")
        s_stats = sem("stats_made")
        s_std = sem("std_made")
        s_rstd = sem("rstd_made")
        s_x1 = sem("x1_made")
        s_x1k = sem("x1_kept")
        s_x1T = sem("x1T_done")
        s_x1Tc = sem("x1T_copied")
        s_h = sem("h_done")
        s_hc = sem("h_copied")
        s_hst = [sem(f"h_stored{s}") for s in range(2)]
        s_e = sem("e_gathered")
        s_hload = sem("h_landed")
        s_gate = sem("gates_made")
        s_redT = sem("gates_transposed")
        s_top = sem("extremes_made")
        s_vord = sem("verdict_steps")
        s_neg = sem("shift_made")
        s_flag = sem("flag_made")
        s_bc = sem("shift_broadcast")
        s_shift = sem("shift_copied")
        s_w = sem("weights_made")
        s_wh = sem("weighted_made")
        s_hi1 = sem("weighted_hi_made")
        s_lo1 = sem("weighted_lo_made")
        s_pkld = [sem(f"packed_landed{s}") for s in range(2)]
        s_unp = sem("unpacked")
        s_sum1 = sem("sum1_done")
        s_lo1c = sem("sum1_lo_copied")
        s_sum1r = sem("sum1_read")
        s_rden = sem("rdenominator_made")
        s_z1 = sem("z1_made")
        s_bn1 = sem("bn1_made")
        s_st1 = sem("stats1_made")
        s_std1 = sem("std1_made")
        s_rstd1 = sem("rstd1_made")
        s_out = sem("out_made")
        s_outst = [sem(f"out_stored{s}") for s in range(2)]

        g_landed = sem("g_adj_landed")
        g_matl = sem("g_matrix_landed")
        g_ones = sem("g_ones_filled")
        g_made = sem("g_rows_made")
        g_masked = sem("g_exponents_masked")
        g_exp = sem("g_exp_made")
        g_T = sem("g_blocks_transposed")
        g_Tc = sem("g_blocks_copied")
        g_used = sem("g_blocks_used")
        g_sum = sem("g_sum_done")
        g_agg = sem("g_agg_made")
        g_xrow = sem("g_x_row_landed")
        g_catT = sem("g_catT_done")
        g_catTc = sem("g_catT_copied")
        g_y = sem("g_y_done")
        g_stats = sem("g_stats_made")
        g_std = sem("g_std_made")
        g_x1 = sem("g_x1_made")
        g_x1T = sem("g_x1T_done")
        g_x1Tc = sem("g_x1T_copied")
        g_h = sem("g_h_done")
        g_hc = sem("g_h_copied")
        g_hst = sem("g_h_stored")
        g_out = sem("g_out_made")
        g_outst = sem("g_out_stored")
        g_chain = [sem(f"g_vector_steps{layer}") for layer in range(2)]
        g_done = sem("g_tile_done")

        block = ctx.enter_context(nc.Block())

        def before(eng, layer, t):
            if layer == 1 and not isinstance(t, int):
                eng.wait_ge(g_out, t)
            else:
                wait(eng, g_done, TILES * layer + t)

        def general_loop(eng, step):
            for layer in range(2):
                step(layer, 0)
                with eng.Fori(1, TILES) as t:
                    step(layer, t)

        def wait(eng, semaphore, count):
            if not isinstance(count, int) or count > 0:
                eng.wait_ge(semaphore, count)

        def wait_apart(eng, *waits):
            waits = [(semaphore, count if isinstance(count, int) else eng.to_reg(count)) for semaphore, count in waits]
            eng.wait_ge(s_fill, 1)
            for semaphore, count in waits:
                wait(eng, semaphore, count)

        def on(t, lag):
            return not isinstance(t, int) or 0 <= t - lag < TILES

        def contract(eng, bank, slot, cols, blocks):
            rows = edgesT[:, slot, :].bitcast(fp8).rearrange("p (b i c) -> p b c i", b=NB, c=BYTES)
            for n in blocks:
                last = eng.matmul(ps_agg[bank][:, 0:cols], rows[:, n // BYTES, n % BYTES, :], parts[:, n, 0:cols],
                                  start=(n == 0), stop=(n == NBLK - 1))
            return last

        @block.sync
        def _(sp):
            for a in range(NQ):
                sp.dma_start(x_stage[QUAD * a:QUAD * (a + 1), :, :].rearrange("p (b c) f -> p b (c f)", c=BYTES),
                             x_quarters[a]).then_inc(s_xload, 16)

            def load_tile(g, k):
                for half in range(2):
                    slot = 2 * k + half
                    wait(sp, s_conv, g * SLOTS + slot - SLOTS + 1)
                    for a in range(NQ):
                        sp.dma_start(adj_in[QUAD * a:QUAD * (a + 1), slot, :, :],
                                     adj_halves[g * SLOTS + slot, a]).then_inc(s_adj[slot], 16)

            for k in range(2):
                load_tile(0, k)
            with sp.Fori(1, TILES // 2) as g:
                for k in range(2):
                    load_tile(g, k)

            for s in range(2):
                sp.wait_ge(s_hst[s], 16 * TILES // 2)
            sp.wait_ge(s_conv, 2 * TILES)
            for a in range(NQ):
                sp.dma_start(stage[QUAD * a:QUAD * (a + 1), :, :].rearrange("p (b c) f -> p b (c f)", c=BYTES),
                             h_quarters[a]).then_inc(s_hload, 16)

            sp.wait_ge(s_flag, 1)
            general = sp.value_load(flag[0:1, 0:1], min_val=0, max_val=1)
            with sp.If(general == 0):
                sp.wait_ge(s_pkst, 16 * GROUPS)

                def load_group(g, s):
                    sp.dma_start(packed_in[:, s, :], packed_dram[g]).then_inc(s_pkld[s], 16)

                for s in range(2):
                    load_group(s, s)
                with sp.Fori(1, GROUPS // 2) as g:
                    for s in range(2):
                        sp.wait_ge(s_unp, GROUP * (2 * g + s - 1))
                        load_group(2 * g + s, s)
            with sp.Else():
                def step(layer, t):
                    u = TILES * layer + t
                    before(sp, layer, t)
                    if isinstance(t, int) and layer == 0:
                        sp.wait_ge(s_lo1, QS)
                        sp.dma_start(g_mat[:, :, 0:F], x.rearrange("(n p) f -> p n f", p=P)).then_inc(g_matl, 16)
                    if isinstance(t, int) and layer == 1:
                        sp.wait_ge(g_hst, 32 * TILES)
                        sp.dma_start(g_mat[:, :, 0:F], h_dram[:, 0:F].rearrange("(n p) f -> p n f", p=P))\
                            .then_inc(g_matl, 16)
                        for half in range(2):
                            sp.dma_start(g_e[half], e_halves[half].to_broadcast([P, N // 2])).then_inc(g_matl, 16)
                    sp.dma_start(g_adj, adj_tiles[t]).then_inc(g_landed, 16)
                    if layer == 0:
                        sp.dma_start(x_row[:, 0, :], x_tiles[t]).then_inc(g_xrow, 16)

                general_loop(sp, step)

        @block.scalar
        def _(act):
            act.dma_start(w1_sb[:, :], w1).then_inc(s_const, 16)
            act.dma_start(w0_sb[:, :, :], w0.rearrange("(c p) f -> p c f", p=P)).then_inc(s_const, 16)
            act.dma_start(a2_sb[:, :], a1[F:2 * F].rearrange("(p o) -> p o", o=1)).then_inc(s_const, 16)
            act.dma_start(bias[:, :], b0.rearrange("(o f) -> o f", o=1).to_broadcast([P, F])).then_inc(s_const, 16)
            act.wait_ge(s_w1T, 1)
            act.activation(w1T[:, 0:F + 1], ps_small[:, 0:F + 1], ACT.Copy).then_inc(s_w1Tc, 1)
            act.wait_ge(s_fill, 1)
            act.wait_ge(s_xload, 16 * NQ)
            for q in range(4):
                blk = slice(q * NBLK // 4, (q + 1) * NBLK // 4)
                act.activation(parts[:, blk, 0:F], x_stage[:, blk, :], ACT.Copy, scale=XSCALE).then_inc(s_hi0, 1)

            def convert(g, k, half):
                t, n = GROUP * g + k, 2 * k + half
                wait_apart(act, (s_adj[n % SLOTS], 16 * NQ * (2 * g + n // SLOTS + 1)),
                           (s_tr, t - 1))
                act.activation(edges[:, k % 2, 2 * half:2 * half + 2, :], adj_in[:, n % SLOTS, :, :], ACT.Copy,
                               scale=2.0 if k == GROUP - 1 else 1.0, saturate=False).then_inc(s_conv, 1)

            def step(g, k):
                t = GROUP * g + k
                if on(t, 3):
                    act.wait_ge(s_stats, t - 2)
                    act.activation(std[:, 0:1], mean_var[:, 1:2], ACT.Sqrt, bias=eps[:, :]).then_inc(s_std, 1)
                if on(t, 0):
                    convert(g, k, 0)
                if on(t, 2):
                    act.wait_ge(s_catT, t - 1)
                    wait(act, s_y, t - 3)
                    act.activation(catT[:, k % 2, :], ps_catT[:, 0:2 * P], ACT.Copy).then_inc(s_catTc, 1)
                if on(t, 4):
                    act.wait_ge(s_x1T, t - 3)
                    wait(act, s_h, t - 5)
                    act.activation(x1T[:, k % 2, :], ps_x1T[:, 0:P], ACT.Copy).then_inc(s_x1Tc, 1)
                if on(t, 0):
                    convert(g, k, 1)
                if on(t, 4):
                    act.wait_ge(s_h, t - 3)
                    wait(act, s_e, t - 5)
                    wait(act, s_hst[k % 2], 16 * (2 * g + (k - 4) // 2))
                    act.activation(h_row[:, k % 2, :], ps_h[:, 0:HCOLS], ACT.Copy).then_inc(s_hc, 1)

            for t in range(2 * GROUP):
                step(t // GROUP, t % GROUP)
            with act.Fori(2, GROUPS) as g:
                for k in range(GROUP):
                    step(g, k)
            for k in range(4):
                step(GROUPS, k)

            act.wait_ge(s_hload, 16 * NQ)
            act.wait_ge(s_shift, 1)
            act.activation(stage[:, :, F], stage[:, :, F], ACT.Exp, bias=shift[:, :]).then_inc(s_w, 1)
            for q in range(QS):
                blk = slice(q * NBLK // QS, (q + 1) * NBLK // QS)
                act.wait_ge(s_wh, q + 1)
                act.activation(parts[:, blk, 0:F + 1], stage[:, blk, 0:F + 1], ACT.Copy).then_inc(s_hi1, 1)

            act.wait_ge(s_flag, 1)
            general = act.value_load(flag[0:1, 0:1], min_val=0, max_val=1)
            with act.If(general == 0):
                def step1(t, k):
                    act.wait_ge(s_sum1, t + 1)
                    act.activation(agg_lo[:, 0:F + 1], ps_agg[k % 2][:, LO:LO + F + 1], ACT.Copy).then_inc(s_lo1c, 1)
                    act.wait_ge(s_st1, t + 1)
                    act.activation(std[:, 0:1], mean_var[:, 1:2], ACT.Sqrt, bias=eps[:, :]).then_inc(s_std1, 1)

                with act.Fori(0, TILES // 2) as g:
                    for k in range(2):
                        step1(2 * g + k, k)
            with act.Else():
                def step(layer, t):
                    u = TILES * layer + t
                    if layer == 1:
                        act.wait_ge(g_masked, t + 1)
                        act.activation(g_rows, g_rows, ACT.Exp, bias=shift[:, :]).then_inc(g_exp, 1)
                    for c in range(NBLK // 4):
                        act.wait_ge(g_T, NBLK // 4 * u + c + 1)
                        wait(act, g_used, NBLK // 4 * u + c - 1)
                        act.activation(g_blockT[:, c % 2, :], g_banks[c % 2][:, :], ACT.Copy).then_inc(g_Tc, 1)
                    if layer == 0:
                        act.wait_ge(g_catT, t + 1)
                        act.activation(catT[:, 0, :], ps_catT[:, 0:2 * P], ACT.Copy).then_inc(g_catTc, 1)
                    act.wait_ge(g_stats, u + 1)
                    act.activation(std[:, 0:1], mean_var[:, 1:2], ACT.Sqrt, bias=eps[:, :]).then_inc(g_std, 1)
                    if layer == 0:
                        act.wait_ge(g_x1T, t + 1)
                        act.activation(x1T[:, 0, :], ps_x1T[:, 0:P], ACT.Copy).then_inc(g_x1Tc, 1)
                        act.wait_ge(g_h, t + 1)
                        wait(act, g_hst, 32 * t)
                        act.activation(h_row[:, 0, :], ps_h[:, 0:HCOLS], ACT.Copy).then_inc(g_hc, 1)

                general_loop(act, step)

        @block.tensor
        def _(pe):
            pe.wait_ge(s_fill, 1)
            pe.wait_ge(s_const, 16 * 4)
            pe.transpose(ps_small[:, 0:P], w1_sb[:, :], ident[:, :])
            pe.matmul(ps_small[:, F:F + 1], w1_sb[:, :], a2_sb[:, :], start=True, stop=True).then_inc(s_w1T, 1)
            pe.wait_ge(s_lo0, 4)
            pe.wait_ge(s_w1Tc, 1)

            def step(g, k):
                t = 2 * g + k
                if on(t, 0):
                    wait_apart(pe, (s_tr, t + 1), (s_aggr, t - 1))
                    contract(pe, k, k, 2 * F + 1, range(0, NBLK // 2))
                if on(t, 1):
                    pe.wait_ge(s_aggr, t)
                    pe.wait_ge(s_xrow[(k - 1) % 2], 16 * (g + (k - 1) // 2 + 1))
                    wait(pe, s_catTc, t - 1)
                    pe.transpose(ps_catT[:, 0:P], agg[:, (k - 1) % 2, :], ident[:, :])
                    pe.transpose(ps_catT[:, P:2 * P], x_row[:, (k - 1) % 2, :], ident[:, :]).then_inc(s_catT, 1)
                if on(t, 3):
                    pe.wait_ge(s_x1, t - 2)
                    wait(pe, s_x1Tc, t - 3)
                    pe.transpose(ps_x1T[:, 0:P], x1_row[:, (k - 3) % 2, :], ident[:, :]).then_inc(s_x1T, 1)
                if on(t, 0):
                    contract(pe, k, k, 2 * F + 1, range(NBLK // 2, NBLK)).then_inc(s_agg, 1)
                if on(t, 1):
                    pe.wait_ge(s_catTc, t)
                    wait(pe, s_z, t - 1)
                    pe.matmul(ps_y[:, 0:F], catT[:, (k - 1) % 2, 0:P], w0_sb[:, 0, :], start=True, stop=False)
                    pe.matmul(ps_y[:, 0:F], catT[:, (k - 1) % 2, P:2 * P], w0_sb[:, 1, :],
                              start=False, stop=True).then_inc(s_y, 1)
                if on(t, 3):
                    pe.wait_ge(s_x1Tc, t - 2)
                    wait(pe, s_hc, t - 3)
                    pe.matmul(ps_h[:, 0:HCOLS], x1T[:, (k - 3) % 2, :], w1T[:, 0:HCOLS],
                              start=True, stop=True).then_inc(s_h, 1)

            for t in range(4):
                step(t // 2, t % 2)
            with pe.Fori(2, TILES // 2) as g:
                for k in range(2):
                    step(g, k)
            for k in range(3):
                step(TILES // 2 + k // 2, k % 2)

            pe.wait_ge(s_gate, 1)
            for c in range(3):
                last = pe.transpose(ps_small[0:1, c * P:(c + 1) * P], gate[:, c:c + 1], ident[:, :])
            last.then_inc(s_redT, 1)
            pe.wait_ge(s_neg, 1)
            pe.matmul(ps_small[:, 0:1], ones[0:1, :], verdict[0:1, 2:3], start=True, stop=True).then_inc(s_bc, 1)

            pe.wait_ge(s_flag, 1)
            general = pe.value_load(flag[0:1, 0:1], min_val=0, max_val=1)
            with pe.If(general == 0):
                def step1(t, k, first):
                    wait_apart(pe, (s_unp, t + 1), (s_sum1r, t - 1))
                    for q in range(QS):
                        if first:
                            pe.wait_ge(s_lo1, q + 1)
                        last = contract(pe, k, k, XCOLS, range(q * NBLK // QS, (q + 1) * NBLK // QS))
                    last.then_inc(s_sum1, 1)

                for t in range(2):
                    step1(t, t, t == 0)
                with pe.Fori(1, TILES // 2) as g:
                    for k in range(2):
                        step1(2 * g + k, k, False)
            with pe.Else():
                def step(layer, t):
                    u = TILES * layer + t
                    pe.wait_ge(g_made, u + 1)
                    if isinstance(t, int):
                        pe.wait_ge(g_matl, 16 * (1 + 3 * layer))
                        pe.wait_ge(g_ones, 1)

                    def blocks_product(c):
                        pe.wait_ge(g_Tc, NBLK // 4 * u + c + 1)
                        for b in range(4):
                            n = 4 * c + b
                            last = pe.matmul(ps_agg[0][:, 0:HCOLS], g_blockT[:, c % 2, b * P:(b + 1) * P],
                                             g_mat[:, n, :], start=(n == 0), stop=(n == NBLK - 1))
                        last.then_inc(g_used, 1)
                        return last

                    for c in range(NBLK // 4):
                        wait(pe, g_Tc, NBLK // 4 * u + c - 1)
                        for b in range(4):
                            n = 4 * c + b
                            last = pe.transpose(g_banks[c % 2][:, b * P:(b + 1) * P], g_rows[:, n * P:(n + 1) * P],
                                                ident[:, :])
                        last.then_inc(g_T, 1)
                        if c > 0:
                            blocks_product(c - 1)
                    blocks_product(NBLK // 4 - 1)
                    if layer == 0:
                        pe.wait_ge(g_agg, t + 1)
                        pe.wait_ge(g_xrow, 16 * (t + 1))
                        pe.transpose(ps_catT[:, 0:P], agg[:, 0, :], ident[:, :])
                        pe.transpose(ps_catT[:, P:2 * P], x_row[:, 0, :], ident[:, :]).then_inc(g_catT, 1)
                        pe.wait_ge(g_catTc, t + 1)
                        pe.matmul(ps_y[:, 0:F], catT[:, 0, 0:P], w0_sb[:, 0, :], start=True, stop=False)
                        pe.matmul(ps_y[:, 0:F], catT[:, 0, P:2 * P], w0_sb[:, 1, :],
                                  start=False, stop=True).then_inc(g_y, 1)
                        pe.wait_ge(g_x1, t + 1)
                        pe.transpose(ps_x1T[:, 0:P], x1_row[:, 0, :], ident[:, :]).then_inc(g_x1T, 1)
                        pe.wait_ge(g_x1Tc, t + 1)
                        pe.matmul(ps_h[:, 0:HCOLS], x1T[:, 0, :], w1T[:, 0:HCOLS], start=True, stop=True)\
                            .then_inc(g_h, 1)

                general_loop(pe, step)

        @block.vector
        def _(dve):
            dve.memset(stray[:, :], 0).then_inc(s_stray0, 1)
            for q in range(4):
                blk = slice(q * NBLK // 4, (q + 1) * NBLK // 4)
                dve.wait_ge(s_hi0, q + 1)
                dve.scalar_tensor_tensor(parts[:, blk, LO:LO + F], x_stage[:, blk, :], XSCALE, parts[:, blk, 0:F],
                                         ALU.mult, ALU.subtract).then_inc(s_lo0, 1)
            dve.tensor_reduce(x_big[:, :], x_stage, AX.X, ALU.max, apply_absolute_value=True).then_inc(s_gate0, 1)
            dve.wait_ge(s_const, 16 * 4)
            dve.tensor_tensor(w_sq[:, :], w1_sb[:, :], w1_sb[:, :], ALU.mult).then_inc(s_gate0, 1)
            dve.wait_ge(s_gate0, 2)
            dve.tensor_reduce(gate[:, 4:5], x_big[:, :], AX.X, ALU.max)
            dve.tensor_reduce(gate[:, 5:6], x_big[:, :], AX.X, ALU.min)
            dve.tensor_reduce(gate[:, 6:7], w_sq[:, :], AX.X, ALU.add).then_inc(s_gate0, 1)
            dve.wait_ge(s_gate0, 3)
            dve.tensor_single_scalar(okay[:, 0:1], gate[:, 4:5], X_MAX, ALU.is_le)
            dve.tensor_single_scalar(okay[:, 1:2], gate[:, 5:6], X_MIN, ALU.is_ge)
            dve.tensor_single_scalar(okay[:, 2:3], gate[:, 6:7], W_NORM2, ALU.is_le).then_inc(s_gate0, 1)
            dve.wait_ge(s_fill, 1)

            def step(g, k):
                t = GROUP * g + k
                if on(t, 0):
                    dve.wait_ge(s_conv, 2 * t + 2)
                    wait(dve, s_agg, t - 1)
                    src = edges[:, k % 2, :, :].bitcast(u32).rearrange("p g (b w) -> p g b w", b=NB)
                    dst = edgesT[:, k % 2, :].rearrange("p (b g i) -> p g b i", b=NB, g=GROUP)
                    for r in range(GROUP):
                        last = dve.transpose(dst[:, r], src[:, r])
                    last.then_inc(s_tr, 1)
                if on(t, 1):
                    bank, s = ps_agg[(k - 1) % 2], (k - 1) % 2
                    dve.wait_ge(s_agg, t)
                    wait(dve, s_aggr, t - 1)
                    dve.reciprocal(rcount[:, :], bank[:, COUNT:COUNT + 1]).then_inc(s_rdeg, 1)
                    dve.wait_ge(s_rdeg, t)
                    dve.tensor_scalar(agg_lo[:, 0:F], bank[:, LO:LO + F], rcount[:, :], None, ALU.mult).then_inc(s_aglo, 1)
                    dve.wait_ge(s_aglo, t)
                    wait(dve, s_catT, t - 2)
                    dve.scalar_tensor_tensor(agg[:, s, :], bank[:, 0:F], rcount[:, :], agg_lo[:, 0:F],
                                             ALU.mult, ALU.add).then_inc(s_aggr, 1)
                if on(t, 2):
                    dve.wait_ge(s_y, t - 1)
                    dve.wait_ge(s_xb, t - 1)
                    wait(dve, s_x1, t - 2)
                    dve.tensor_tensor(z[:, :], ps_y[:, 0:F], xb[:, k % 2, :], ALU.add).then_inc(s_z, 1)
                    dve.wait_ge(s_z, t - 1)
                    dve.bn_stats(stats[:, :], z[:, :]).then_inc(s_bn, 1)
                    wait_apart(dve, (s_bn, t - 1))
                    dve.bn_aggr(mean_var[:, :], stats[:, :]).then_inc(s_stats, 1)
                if on(t, 0):
                    dve.wait_ge(s_tr, t + 1)
                    if not isinstance(t, int) or t > 0:
                        dve.wait_ge(s_check, t)
                    dve.scalar_tensor_tensor(stray[:, :], edgesT[:, k % 2, :], every_byte(0xFF ^ EDGE[k]), stray[:, :],
                                             ALU.bitwise_and, ALU.bitwise_or).then_inc(s_check, 1)
                    if k == 0:
                        wait(dve, s_pkst, 16 * g)
                        dve.tensor_single_scalar(packed[:, :], edgesT[:, k % 2, :], every_byte(BIT[k]),
                                                 ALU.bitwise_and).then_inc(s_pack, 1)
                    else:
                        dve.wait_ge(s_pack, t)
                        dve.scalar_tensor_tensor(packed[:, :], edgesT[:, k % 2, :], every_byte(BIT[k]),
                                                 packed[:, :], ALU.bitwise_and, ALU.bitwise_or).then_inc(s_pack, 1)
                if on(t, 2):
                    dve.wait_ge(s_std, t - 1)
                    dve.reciprocal(rstd[:, :], std[:, 0:1]).then_inc(s_rstd, 1)
                    dve.wait_ge(s_rstd, t - 1)
                    wait(dve, s_x1T, t - 3)
                    wait(dve, s_x1k, t - 3)
                    dve.tensor_scalar(x1_row[:, k % 2, :], z[:, :], mean_var[:, 0:1], rstd[:, :],
                                      ALU.subtract, ALU.mult).then_inc(s_x1, 1)

            for k in range(GROUP):
                step(0, k)
            with dve.Fori(1, GROUPS) as g:
                for k in range(GROUP):
                    step(g, k)
            dve.wait_ge(s_check, TILES)
            dve.tensor_reduce(gate[:, 3:4], stray[:, :].bitcast(i32), AX.X, ALU.max,
                              apply_absolute_value=True).then_inc(s_gate0, 1)
            dve.wait_ge(s_gate0, 5)
            dve.tensor_single_scalar(okay[:, 3:4], gate[:, 3:4], 0.0, ALU.is_equal).then_inc(s_gate0, 1)
            dve.wait_ge(s_gate0, 6)
            dve.tensor_reduce(gate[:, 2:3], okay[:, :], AX.X, ALU.min, negate=True)
            for k in range(2):
                step(GROUPS, k)

            dve.wait_ge(s_e, TILES)
            dve.tensor_reduce(gate[:, 0:1], e_all[:, :], AX.X, ALU.max)
            dve.tensor_reduce(gate[:, 1:2], e_all[:, :], AX.X, ALU.min, negate=True).then_inc(s_gate, 1)
            dve.wait_ge(s_redT, 1)
            dve.tensor_reduce(top[0:1, :], ps_small[0:1, 0:3 * P].rearrange("o (c p) -> o c p", p=P), AX.X,
                              ALU.max).then_inc(s_top, 1)
            dve.wait_ge(s_top, 1)
            dve.tensor_scalar(verdict[0:1, 2:3], top[0:1, 0:1], -1.0, W_SHIFT, ALU.mult, ALU.add).then_inc(s_neg, 1)
            dve.tensor_tensor(verdict[0:1, 0:1], top[0:1, 0:1], top[0:1, 1:2], ALU.add).then_inc(s_vord, 1)
            dve.wait_ge(s_bc, 1)
            dve.tensor_copy(shift[:, :], ps_small[:, 0:1]).then_inc(s_shift, 1)
            dve.wait_ge(s_vord, 1)
            dve.tensor_scalar(verdict[0:1, 1:2], verdict[0:1, 0:1], E_SPAN, top[0:1, 2:3], ALU.is_le, ALU.mult).then_inc(s_vord, 1)
            dve.wait_ge(s_vord, 2)
            dve.tensor_scalar(flag[0:1, :], verdict[0:1, 1:2], 1.0, None, ALU.add).then_inc(s_flag, 1)

            dve.wait_ge(s_w, 1)
            for q in range(QS):
                blk = slice(q * NBLK // QS, (q + 1) * NBLK // QS)
                dve.tensor_tensor(stage[:, blk, 0:F], stage[:, blk, 0:F],
                                  stage[:, blk, F:F + 1].to_broadcast([P, NBLK // QS, F]), ALU.mult).then_inc(s_wh, 1)
                dve.wait_ge(s_hi1, q + 1)
                dve.tensor_tensor(parts[:, blk, LO:LO + F + 1], stage[:, blk, :], parts[:, blk, 0:F + 1],
                                  ALU.subtract).then_inc(s_lo1, 1)

            general = dve.value_load(flag[0:1, 0:1], min_val=0, max_val=1)
            with dve.If(general == 0):
                def unpack(g, m, k):
                    t = 2 * GROUP * g + GROUP * m + k
                    if k == 0:
                        dve.wait_ge(s_pkld[m], 16 * (g + 1))
                    wait(dve, s_sum1, t - 1)
                    dve.tensor_single_scalar(edgesT[:, k % 2, :], packed_in[:, m, :], every_byte(BIT[k]),
                                             ALU.bitwise_and).then_inc(s_unp, 1)

                def rows_out(t, k, gg):
                    s = k % 2
                    bank = ps_agg[s]
                    dve.wait_ge(s_lo1c, t + 1)
                    wait(dve, s_out, t)
                    dve.tensor_tensor(zsum[:, :], bank[:, 0:F + 1], agg_lo[:, 0:F + 1], ALU.add).then_inc(s_sum1r, 1)
                    dve.wait_ge(s_sum1r, t + 1)
                    dve.reciprocal(rcount[:, :], zsum[:, COUNT:COUNT + 1]).then_inc(s_rden, 1)
                    dve.wait_ge(s_rden, t + 1)
                    dve.scalar_tensor_tensor(z[:, :], zsum[:, 0:F], rcount[:, :], x1[:, t, :],
                                             ALU.mult, ALU.add).then_inc(s_z1, 1)
                    dve.wait_ge(s_z1, t + 1)
                    dve.bn_stats(stats[:, :], z[:, :]).then_inc(s_bn1, 1)
                    wait_apart(dve, (s_bn1, t + 1))
                    dve.bn_aggr(mean_var[:, :], stats[:, :]).then_inc(s_st1, 1)
                    dve.wait_ge(s_std1, t + 1)
                    dve.reciprocal(rstd[:, :], std[:, 0:1]).then_inc(s_rstd1, 1)
                    dve.wait_ge(s_rstd1, t + 1)
                    wait(dve, s_outst[s], 16 * (4 * gg + k // 2))
                    dve.tensor_scalar(y_out[:, s, :], z[:, :], mean_var[:, 0:1], rstd[:, :],
                                      ALU.subtract, ALU.mult).then_inc(s_out, 1)

                def body1(g):
                    for j in range(2 * GROUP):
                        unpack(g, j // GROUP, j % GROUP)
                        t = 2 * GROUP * g + j - 1
                        if not isinstance(t, int) or t >= 0:
                            rows_out(t, j - 1, g)

                dve.wait_ge(s_x1k, TILES)
                body1(0)
                with dve.Fori(1, GROUPS // 2) as g:
                    body1(g)
                rows_out(TILES - 1, -1, GROUPS // 2)

            with dve.Else():
                def step(layer, t):
                    u = TILES * layer + t
                    steps = 5 if layer == 0 else 7
                    n = [0]

                    def link(ins):
                        n[0] += 1
                        ins.then_inc(g_chain[layer], 1)
                        wait_apart(dve, (g_chain[layer], steps * t + n[0]))

                    dve.wait_ge(g_landed, 16 * (u + 1))
                    before(dve, layer, t)
                    if layer == 0:
                        dve.tensor_copy(g_rows, g_adj).then_inc(g_made, 1)
                    else:
                        if isinstance(t, int):
                            dve.wait_ge(g_matl, 16 * 4)
                        link(dve.tensor_scalar(g_rows, g_adj, 0.0, -1e38, ALU.is_equal, ALU.mult))
                        for half in range(2):
                            part = g_rows[:, half * N // 2:(half + 1) * N // 2]
                            last = dve.tensor_tensor(part, part, g_e[half], ALU.add)
                        link(last)
                        link(dve.tensor_reduce(top_row[:, :], g_rows, AX.X, ALU.max))
                        dve.tensor_scalar(shift[:, :], top_row[:, :], -1.0, None, ALU.mult).then_inc(g_masked, 1)
                        dve.wait_ge(g_exp, t + 1)
                        dve.scalar_tensor_tensor(g_rows, g_adj, 0.0, g_rows, ALU.not_equal, ALU.mult)\
                            .then_inc(g_made, 1)
                    dve.wait_ge(g_used, NBLK // 4 * (u + 1))
                    link(dve.reciprocal(rcount[:, :], ps_agg[0][:, COUNT:COUNT + 1]))
                    if layer == 0:
                        dve.tensor_scalar(agg[:, 0, :], ps_agg[0][:, 0:F], rcount[:, :], None, ALU.mult).then_inc(g_agg, 1)
                        dve.wait_ge(g_y, t + 1)
                        link(dve.tensor_tensor(z[:, :], ps_y[:, 0:F], bias[:, :], ALU.add))
                        link(dve.tensor_tensor(z[:, :], z[:, :], x_row[:, 0, :], ALU.add))
                    else:
                        link(dve.scalar_tensor_tensor(z[:, :], ps_agg[0][:, 0:F], rcount[:, :], x1[:, t, :],
                                                      ALU.mult, ALU.add))
                    link(dve.bn_stats(stats[:, :], z[:, :]))
                    dve.bn_aggr(mean_var[:, :], stats[:, :]).then_inc(g_stats, 1)
                    dve.wait_ge(g_std, u + 1)
                    link(dve.reciprocal(rstd[:, :], std[:, 0:1]))
                    if layer == 0:
                        dve.tensor_scalar(x1_row[:, 0, :], z[:, :], mean_var[:, 0:1], rstd[:, :],
                                          ALU.subtract, ALU.mult).then_inc(g_x1, 1)
                        dve.wait_ge(g_x1, t + 1)
                        dve.wait_ge(g_hc, t + 1)
                        dve.tensor_copy(x1[:, t, :], x1_row[:, 0, :]).then_inc(g_done, 1)
                    else:
                        wait(dve, g_outst, 16 * t)
                        dve.tensor_scalar(y_out[:, 0, :], z[:, :], mean_var[:, 0:1], rstd[:, :],
                                          ALU.subtract, ALU.mult).then_inc(g_out, 1)
                    assert n[0] == steps, n[0]

                dve.wait_ge(s_lo1, QS)
                general_loop(dve, step)

        @block.gpsimd
        def _(pool):
            pool.memset(ident[:, :], 0.0).then_inc(s_id, 1)
            pool.memset(ones[:, :], 1.0)
            pool.memset(eps[:, :], EPS)
            pool.memset(parts[:, :, COUNT:COUNT + 1], XSCALE)
            pool.wait_ge(s_id, 1)
            pool.affine_select(out=ident[:, :], in_=ident[:, :], compare_op=ALU.not_equal, fill=1.0, base=0,
                               pattern=[[-1, P]], channel_multiplier=1).then_inc(s_fill, 1)
            pool.wait_ge(s_const, 16 * 4)

            def step(g, k):
                t = 2 * g + k
                if on(t, 0):
                    wait(pool, s_catT, t - 1)
                    wait(pool, s_xb, t - 1)
                    pool.dma_start(x_row[:, k, :], x_tiles[t]).then_inc(s_xrow[k], 16)
                if on(t, 3):
                    pool.wait_ge(s_x1, t - 2)
                    pool.tensor_copy(x1[:, t - 3, :], x1_row[:, (k - 3) % 2, :]).then_inc(s_x1k, 1)
                if on(t, 4):
                    pool.wait_ge(s_hc, t - 3)
                    pool.dma_start(h_tiles[t - 4], h_row[:, k, :]).then_inc(s_hst[k], 16)
                    pool.tensor_copy(e_all[:, bass.ds(t - 4, 1)], h_row[:, k, F:F + 1]).then_inc(s_e, 1)
                if on(t, 0):
                    pool.wait_ge(s_xrow[k], 16 * (g + 1))
                    wait(pool, s_z, t - 1)
                    pool.tensor_tensor(xb[:, k, :], x_row[:, k, :], bias[:, :], ALU.add).then_inc(s_xb, 1)

            def store_group(g):
                pool.wait_ge(s_pack, GROUP * (g + 1))
                pool.dma_start(packed_dram[g], packed[:, :]).then_inc(s_pkst, 16)

            for k in range(GROUP):
                step(k // 2, k % 2)
            with pool.Fori(1, GROUPS) as g:
                step(2 * g, 0)
                store_group(g - 1)
                step(2 * g, 1)
                step(2 * g + 1, 0)
                step(2 * g + 1, 1)
            store_group(GROUPS - 1)
            for k in range(4):
                step(TILES // 2 + k // 2, k % 2)

            pool.wait_ge(s_flag, 1)
            general = pool.value_load(flag[0:1, 0:1], min_val=0, max_val=1)
            with pool.If(general == 0):
                def store_rows(t, s):
                    pool.wait_ge(s_out, t + 1)
                    pool.dma_start(out_tiles[t], y_out[:, s, :]).then_inc(s_outst[s], 16)

                with pool.Fori(0, TILES // 2) as g:
                    for s in range(2):
                        store_rows(2 * g + s, s)
                for s in range(2):
                    pool.wait_ge(s_outst[s], 16 * TILES // 2)
            with pool.Else():
                pool.wait_ge(s_lo1, QS)
                pool.memset(g_mat[:, :, F:F + 1], 1.0).then_inc(g_ones, 1)

                def step(layer, t):
                    if layer == 0:
                        pool.wait_ge(g_hc, t + 1)
                        pool.dma_start(h_tiles[t], h_row[:, 0, :]).then_inc(g_hst, 16)
                        pool.dma_start(e_tiles[t], h_row[:, 0, F:F + 1]).then_inc(g_hst, 16)
                    else:
                        pool.wait_ge(g_out, t + 1)
                        pool.dma_start(out_tiles[t], y_out[:, 0, :]).then_inc(g_outst, 16)

                general_loop(pool, step)
                pool.wait_ge(g_outst, 16 * TILES)


_INS = ['x', 'adj', 'L0_gnn_weight', 'L0_gnn_bias', 'L1_gnn_W', 'L1_gnn_a']


def kernel(**inputs):
    import numpy as _np
    import concourse.bacc as _bacc
    from concourse import mybir as _mybir
    from concourse.bass_utils import run_bass_kernel_spmd as _run

    nc = _bacc.Bacc("TRN2", target_bir_lowering=False, num_devices=1)
    arrays, args = {}, []
    for name in _INS:
        a = _np.ascontiguousarray(inputs[name])
        arrays[f"in_{name}_dram"] = a
        args.append(nc.dram_tensor(f"in_{name}_dram", a.shape, _mybir.dt.from_np(a.dtype), kind="ExternalInput").ap())
    out_shape = inputs['x'].shape
    args.append(nc.dram_tensor("out_0_dram", out_shape, _mybir.dt.float32, kind="ExternalOutput").ap())
    bass_two_graph_layers(nc, *args)
    r = _run(nc, [arrays], core_ids=[0])
    return r.results[0]["out_0_dram"]
```

```python
import math
from contextlib import ExitStack

import concourse.bass as bass
from concourse import mybir


def bass_two_graph_layers(
    nc: bass.Bass,
    x: bass.AP,
    adj: bass.AP,
    w0: bass.AP,
    b0: bass.AP,
    w1: bass.AP,
    a1: bass.AP,
    out: bass.AP,
):
    fp32, fp16, fp8 = mybir.dt.float32, mybir.dt.float16, mybir.dt.float8e4
    i32, u32 = mybir.dt.int32, mybir.dt.uint32
    ALU, ACT, AX = mybir.AluOpType, mybir.ActivationFunctionType, mybir.AxisListType

    N, F = x.shape
    P = 128
    QUAD = 32
    NQ = P // QUAD
    BYTES = 4
    BANDS = 4
    JB = N // BANDS
    JQ = N // NQ
    NB = JQ // (QUAD * BYTES)
    NBLK = NB * BYTES
    BBLK = NBLK // BANDS
    TILES = N // P
    BTILES = TILES // BANDS
    GROUP = 4
    GROUPS = TILES // GROUP
    TW = NB * P
    BW = TW // BANDS
    SLOTS = 4
    CHECKS = 4
    HCOLS = F + 1
    XCOLS = 2 * F + 2
    LO = F + 1
    COUNT = F
    DELAY = 8
    EARLY = BTILES + DELAY
    SHIFT_GROUP = BTILES // GROUP + 1

    def bands_of(g):
        return max(0, (GROUP * g - DELAY) // BTILES)

    XSCALE = 4096.0
    X_MAX, X_MIN = 15.0, 2.0 ** -14
    W_SHIFT = 8.0 * math.log(2.0)
    E_ABOVE = 3.0 * math.log(2.0)
    W_CAP = W_SHIFT + E_ABOVE + 0.01
    E_BELOW = 7.0
    W_NORM2 = 7.0
    EPS = 1e-5
    EDGE = [0x38, 0x38, 0x38, 0x40]
    BIT = [0x08, 0x10, 0x20, 0x40]
    BIT_SCALE = [2.0 ** -6, 2.0 ** -5, 2.0 ** -3, 1.0]

    def every_byte(b):
        return b * 0x01010101

    packed_dram = nc.dram_tensor("packed_adj", (GROUPS, P, TW), u32, kind="Internal").ap()
    h_dram = nc.dram_tensor("h_rows", (N, HCOLS), fp32, kind="Internal").ap()
    x1_dram = nc.dram_tensor("x1_rows", (N, F), fp32, kind="Internal").ap()
    e_dram = nc.dram_tensor("e_row", (TILES, P), fp32, kind="Internal").ap()

    x_bands = x.rearrange("(s a b p c) f -> s a p b (c f)", s=BANDS, a=NQ, p=QUAD, c=BYTES)
    h_bands = h_dram.rearrange("(s a b p c) f -> s a p b (c f)", s=BANDS, a=NQ, p=QUAD, c=BYTES)
    adj_halves = adj.rearrange("(n g q) (s a j) -> n a g q s j", g=2, q=QUAD, s=BANDS, a=NQ)
    adj_tiles = adj.rearrange("(t p) j -> t p j", p=P)
    x_tiles = x.rearrange("(t p) f -> t p f", p=P)
    h_tiles = h_dram.rearrange("(t p) f -> t p f", p=P)
    x1_tiles = x1_dram.rearrange("(t p) f -> t p f", p=P)
    x1_groups = x1_dram.rearrange("(g k p) f -> g p k f", k=GROUP, p=P)
    e_tiles = e_dram.rearrange("t (p o) -> t p o", o=1)
    e_row = e_dram.rearrange("(o t) p -> o (t p)", o=1)
    out_tiles = out.rearrange("(t p) f -> t p f", p=P)

    ctx = ExitStack()
    with ctx:
        def sb(name, shape, dt):
            return ctx.enter_context(nc.sbuf_tensor(name, shape, dt))

        def ps(name):
            return ctx.enter_context(nc.psum_tensor(name, [P, 512], fp32))

        def sem(name):
            return ctx.enter_context(nc.semaphore(name))

        adj_in = sb("adj_in", [P, SLOTS, 2, JQ], i32)
        edges = sb("edges", [P, 2, 2, JQ], fp8)
        edgesT = sb("edgesT", [P, 2, TW], u32)
        packed = sb("packed", [P, 2, TW], u32)
        parts0 = sb("parts0", [P, NBLK, XCOLS], fp16)
        parts1 = sb("parts1", [P, NBLK, XCOLS], fp16)
        partial = sb("partial", [P, TILES - EARLY, HCOLS], fp32)
        stray = sb("stray", [P, TW // CHECKS], u32)
        x_row = sb("x_row", [P, 4, F], fp32)
        xb = sb("xb", [P, 2, F], fp32)
        agg_lo = sb("agg_lo", [P, F + 1], fp32)
        part_lo = sb("part_lo", [P, F + 1], fp32)
        agg = sb("agg", [P, 2, F], fp32)
        catT = sb("catT", [P, 2, 2 * P], fp32)
        z = sb("z", [P, 1, F], fp32)
        z1 = agg
        zsum = part_lo
        stats = sb("stats", [P, 6], fp32)
        mean_var = sb("mean_var", [P, 2, 2], fp32)
        std = sb("std", [P, 2], fp32)
        rstd = sb("rstd", [P, 1], fp32)
        rcount = sb("rcount", [P, 1], fp32)
        x1_row = sb("x1_row", [P, 4, F], fp32)
        x1T = sb("x1T", [P, 2, P], fp32)
        h_row = sb("h_row", [P, 4, HCOLS], fp32)
        e_all = sb("e_all", [P, TILES], fp32)
        y_out = x1_row
        w0_sb = sb("w0_sb", [P, 2, F], fp32)
        w1_sb = sb("w1_sb", [P, F], fp32)
        w1T = sb("w1T", [P, HCOLS], fp32)
        a2_sb = sb("a2_sb", [P, 1], fp32)
        bias = sb("bias", [P, F], fp32)
        ident = sb("ident", [P, P], fp32)
        ones = sb("ones", [1, P], fp32)
        eps = sb("eps", [P, 1], fp32)
        x_big = sb("x_big", [P, NBLK], fp32)
        gate = sb("gate", [P, 8], fp32)
        okay = sb("okay", [P, 4], fp32)
        top = sb("top", [1, 4], fp32)
        verdict = sb("verdict", [1, 4], fp32)
        flag = sb("flag", [1, 1], i32)
        shift = sb("shift", [P, 1], fp32)
        top_row = sb("top_row", [P, 1], fp32)

        x_stage = parts1[:, :, :].rearrange("p n f -> p (n f)").bitcast(fp32)[:, 0:NBLK * F]\
            .rearrange("p (n f) -> p n f", f=F)
        adj_flat = adj_in[:, :, :, :].rearrange("p s g j -> p (s g j)")
        packed_in = adj_flat[:, 0:2 * TW].bitcast(u32).rearrange("p (s w) -> p s w", s=2)
        x1_in = adj_flat[:, 2 * TW:2 * TW + 2 * GROUP * F].bitcast(fp32)\
            .rearrange("p (s k f) -> p s k f", s=2, k=GROUP)

        def h_stage(s):
            if s < BANDS - 1:
                mem = parts1[:, (s + 1) * BBLK:(s + 2) * BBLK, :].rearrange("p n f -> p (n f)").bitcast(fp32)
            else:
                mem = adj_flat[:, 3 * TW:3 * TW + BBLK * HCOLS].bitcast(fp32)
            return mem.rearrange("p (n f) -> p n f", f=HCOLS)

        g_adj = adj_flat[:, 0:N]
        g_rows = adj_flat[:, N:2 * N].bitcast(fp32)
        g_mat = parts1[:, :, :].rearrange("p n f -> p (n f)").bitcast(fp32).rearrange("p (n f) -> p n f", f=HCOLS)
        g_e = parts0[:, :, :].rearrange("p n f -> p (n f)").bitcast(fp32)[:, 0:N]
        g_blockT = edgesT[:, 0, 0:8 * P].bitcast(fp32).rearrange("p (s i) -> p s i", s=2)

        ps_agg = [ps("ps_agg0"), ps("ps_agg1")]
        ps_part = ps("ps_part")
        ps_catT = ps("ps_catT")
        ps_y = ps("ps_y")
        ps_x1T = ps("ps_x1T")
        ps_h = ps("ps_h")
        ps_small = ps("ps_small")
        g_banks = [ps_agg[1], ps_small]

        s_xload = sem("x_landed")
        s_const = sem("weights_landed")
        s_fill = sem("constants_filled")
        s_id = sem("ident_cleared")
        s_stray0 = sem("stray_cleared")
        s_w1T = sem("w1T_done")
        s_w1Tc = sem("w1T_copied")
        s_hi0 = sem("x_hi_made")
        s_lo0 = sem("x_lo_made")
        s_gate0 = sem("gates0_made")
        s_adj = [sem(f"adj_landed{s}") for s in range(SLOTS)]
        s_conv = sem("half_converted")
        s_trh = sem("half_transposed")
        s_check = sem("checked")
        s_pack = sem("tile_packed")
        s_pkst = sem("packed_stored")
        s_agg = sem("agg_summed")
        s_rdeg = sem("rdegree_made")
        s_aglo = sem("agg_lo_scaled")
        s_aggr = sem("agg_made")
        s_part = sem("partial_summed")
        s_partlo = sem("partial_lo_scaled")
        s_partk = sem("partial_kept")
        s_xrow = [sem(f"x_row_landed{s}") for s in range(4)]
        s_xb = sem("x_plus_bias_made")
        s_catT = sem("catT_done")
        s_catTc = sem("catT_copied")
        s_y = sem("y_done")
        s_z = sem("z_made")
        s_bn = sem("bn_made")
        s_stats = sem("stats_made")
        s_std = sem("std_made")
        s_rstd = sem("rstd_made")
        s_x1 = sem("x1_made")
        s_x1st = [sem(f"x1_stored{s}") for s in range(4)]
        s_x1T = sem("x1T_done")
        s_x1Tc = sem("x1T_copied")
        s_h = sem("h_done")
        s_hc = sem("h_copied")
        s_hst = [sem(f"h_stored{s}") for s in range(4)]
        s_e = sem("e_gathered")
        s_max0 = sem("max_made")
        s_max0T = sem("max_transposed")
        s_top0 = sem("band0_max_made")
        s_neg = sem("shift_made")
        s_bc = sem("shift_broadcast")
        s_shift = sem("shift_copied")
        s_hload = sem("h_landed")
        s_exponent = sem("exponents_made")
        s_w = sem("weights_made")
        s_wh = sem("weighted_made")
        s_hi1 = sem("weighted_hi_made")
        s_lo1 = sem("weighted_lo_made")
        s_gate = sem("gates_made")
        s_redT = sem("gates_transposed")
        s_top = sem("extremes_made")
        s_vord = sem("verdict_steps")
        s_flag = sem("flag_made")
        s_pkld = [sem(f"packed_landed{s}") for s in range(2)]
        s_unp = sem("unpacked")
        s_head = sem("first_bands_summed")
        s_sum1 = sem("sum1_done")
        s_lo1c = sem("sum1_lo_copied")
        s_sum1r = sem("sum1_read")
        s_padd = sem("partial_added")
        s_rden = sem("rdenominator_made")
        s_z1 = sem("z1_made")
        s_bn1 = sem("bn1_made")
        s_st1 = sem("stats1_made")
        s_std1 = sem("std1_made")
        s_rstd1 = sem("rstd1_made")
        s_out = sem("out_made")
        s_outst = [sem(f"out_stored{s}") for s in range(4)]
        g_landed = sem("g_adj_landed")
        g_matl = sem("g_matrix_landed")
        g_ones = sem("g_ones_filled")
        g_made = sem("g_rows_made")
        g_masked = sem("g_exponents_masked")
        g_exp = sem("g_exp_made")
        g_T = sem("g_blocks_transposed")
        g_Tc = sem("g_blocks_copied")
        g_used = sem("g_blocks_used")
        g_agg = sem("g_agg_made")
        g_xrow = sem("g_x_row_landed")
        g_catT = sem("g_catT_done")
        g_catTc = sem("g_catT_copied")
        g_y = sem("g_y_done")
        g_stats = sem("g_stats_made")
        g_std = sem("g_std_made")
        g_x1 = sem("g_x1_made")
        g_x1T = sem("g_x1T_done")
        g_x1Tc = sem("g_x1T_copied")
        g_h = sem("g_h_done")
        g_hc = sem("g_h_copied")
        g_hst = sem("g_rows_stored")
        g_out = sem("g_out_made")
        g_outst = sem("g_out_stored")
        g_chain = [sem(f"g_vector_steps{layer}") for layer in range(2)]

        block = ctx.enter_context(nc.Block())

        def wait(eng, semaphore, count):
            if not isinstance(count, int) or count > 0:
                eng.wait_ge(semaphore, count)

        def wait_apart(eng, *waits):
            waits = [(semaphore, count if isinstance(count, int) else eng.to_reg(count)) for semaphore, count in waits]
            eng.wait_ge(s_fill, 1)
            for semaphore, count in waits:
                wait(eng, semaphore, count)

        def on(t, lag):
            return not isinstance(t, int) or 0 <= t - lag < TILES

        def groups_loop(eng, body, single, per=1):
            g = 0
            while g < GROUPS:
                end = g + per
                while end < GROUPS and g not in single and end not in single and bands_of(end) == bands_of(g):
                    end += per
                if end == g + per:
                    body(g, g)
                else:
                    with eng.Fori(g // per, end // per) as r:
                        body(r * per, g)
                g = end

        def early(g, g0, k, lag):
            return bands_of(g0) > 0 if not isinstance(g, int) else EARLY <= GROUP * g + k - lag < TILES

        def contract(eng, bank, slot, moving, blocks, first, last):
            rows = edgesT[:, slot, :].bitcast(fp8).rearrange("p (b i c) -> p b c i", b=NB, c=BYTES)
            cols = moving.shape[2]
            for n in blocks:
                done = eng.matmul(bank[:, 0:cols], rows[:, n // BYTES, n % BYTES, :], moving[:, n, :],
                                  start=(n == first), stop=(n == last))
            return done

        def general_loop(eng, step):
            for layer in range(2):
                step(layer, 0)
                with eng.Fori(1, TILES) as t:
                    step(layer, t)

        def g_before(eng, layer, t):
            if layer == 0:
                wait(eng, g_hc, t)
            elif isinstance(t, int):
                eng.wait_ge(g_hc, TILES)
            else:
                eng.wait_ge(g_out, t)

        firsts = {g for g in range(1, GROUPS) if bands_of(g) > bands_of(g - 1)}

        @block.sync
        def _(sp):
            for s in range(BANDS):
                for a in range(NQ):
                    sp.dma_start(x_stage[QUAD * a:QUAD * (a + 1), s * BBLK:(s + 1) * BBLK, :]
                                 .rearrange("p (b c) f -> p b (c f)", c=BYTES), x_bands[s, a]).then_inc(s_xload, 16)

            def load_band(s):
                for slot in range(4):
                    sp.wait_ge(s_hst[slot], 16 * BTILES // 4 * (s + 1))
                for a in range(NQ):
                    sp.dma_start(h_stage(s)[QUAD * a:QUAD * (a + 1), :, :].rearrange("p (b c) f -> p b (c f)", c=BYTES),
                                 h_bands[s, a]).then_inc(s_hload, 16)

            def group(g, g0):
                if g0 in firsts:
                    load_band(bands_of(g0) - 1)
                for k in range(GROUP):
                    t = GROUP * g + k
                    for half in range(2):
                        n = 2 * k + half
                        slot = n % SLOTS
                        wait(sp, s_conv, 2 * GROUP * g + n - SLOTS + 1)
                        for a in range(NQ):
                            for r in range(2):
                                sp.dma_start(adj_in[QUAD * a:QUAD * (a + 1), slot, r, :]
                                             .rearrange("p (s j) -> p s j", s=BANDS),
                                             adj_halves[2 * GROUP * g + n, a, r]).then_inc(s_adj[slot], 16)
                    wait(sp, s_catT, t - 3)
                    wait(sp, s_xb, t - 3)
                    sp.dma_start(x_row[:, k, :], x_tiles[t]).then_inc(s_xrow[k], 16)

            groups_loop(sp, group, {0} | firsts)

            def load_group(g, s, bands):
                sp.dma_start(packed_in[:, s, bands * BW:TW], packed_dram[g][:, bands * BW:TW]).then_inc(s_pkld[s], 16)
                sp.dma_start(x1_in[:, s, :, :], x1_groups[g]).then_inc(s_pkld[s], 16)

            sp.wait_ge(s_conv, 2 * TILES)
            sp.wait_ge(s_pkst, 16 * 2)
            for slot in range(4):
                sp.wait_ge(s_x1st[slot], 16 * 2)
            for s in range(2):
                load_group(s, s, 0)
            load_band(BANDS - 1)
            sp.wait_ge(s_pkst, 16 * GROUPS)
            for slot in range(4):
                sp.wait_ge(s_x1st[slot], 16 * TILES // 4)

            sp.wait_ge(s_flag, 1)
            general = sp.value_load(flag[0:1, 0:1], min_val=0, max_val=1)
            with sp.If(general == 0):
                def pair(g, g0):
                    if isinstance(g, int) and g == 0:
                        return
                    for s in range(2):
                        sp.wait_ge(s_z1, GROUP * (g + s - 1))
                        load_group(g + s, s, bands_of(g0))

                groups_loop(sp, pair, {0}, per=2)
            with sp.Else():
                def step(layer, t):
                    g_before(sp, layer, t)
                    if isinstance(t, int) and layer == 0:
                        sp.wait_ge(s_lo1, BANDS)
                        sp.wait_ge(s_head, 4)
                        for s in range(2):
                            sp.wait_ge(s_pkld[s], 16 * 2)
                        sp.dma_start(g_mat[:, :, 0:F], x.rearrange("(n p) f -> p n f", p=P)).then_inc(g_matl, 16)
                    if isinstance(t, int) and layer == 1:
                        sp.wait_ge(g_hst, 48 * TILES)
                        sp.dma_start(g_mat[:, :, 0:F], h_dram[:, 0:F].rearrange("(n p) f -> p n f", p=P))\
                            .then_inc(g_matl, 16)
                        sp.dma_start(g_e, e_row.to_broadcast([P, N])).then_inc(g_matl, 16)
                    sp.dma_start(g_adj, adj_tiles[t]).then_inc(g_landed, 16)
                    sp.dma_start(x_row[:, 0, :], (x_tiles if layer == 0 else x1_tiles)[t]).then_inc(g_xrow, 16)

                general_loop(sp, step)

        @block.scalar
        def _(act):
            act.dma_start(w1_sb[:, :], w1).then_inc(s_const, 16)
            act.dma_start(w0_sb[:, :, :], w0.rearrange("(c p) f -> p c f", p=P)).then_inc(s_const, 16)
            act.dma_start(a2_sb[:, :], a1[F:2 * F].rearrange("(p o) -> p o", o=1)).then_inc(s_const, 16)
            act.dma_start(bias[:, :], b0.rearrange("(o f) -> o f", o=1).to_broadcast([P, F])).then_inc(s_const, 16)
            act.wait_ge(s_w1T, 1)
            act.activation(w1T[:, 0:F + 1], ps_small[:, 0:F + 1], ACT.Copy).then_inc(s_w1Tc, 1)
            act.wait_ge(s_fill, 1)
            act.wait_ge(s_xload, 16 * NQ * BANDS)
            for q in range(4):
                blk = slice(q * NBLK // 4, (q + 1) * NBLK // 4)
                act.activation(parts0[:, blk, 0:F], x_stage[:, blk, :], ACT.Copy, scale=XSCALE).then_inc(s_hi0, 1)

            def convert(g, k, half):
                t, n = GROUP * g + k, 2 * k + half
                wait_apart(act, (s_adj[n % SLOTS], 2 * 16 * NQ * (2 * g + n // SLOTS + 1)),
                           (s_trh, 2 * t + half - 1))
                act.activation(edges[:, half, :, :], adj_in[:, n % SLOTS, :, :], ACT.Copy,
                               scale=2.0 if k == GROUP - 1 else 1.0, saturate=False).then_inc(s_conv, 1)

            def weights(s):
                act.wait_ge(s_exponent, s + 1)
                act.activation(h_stage(s)[:, :, F], h_stage(s)[:, :, F], ACT.Exp).then_inc(s_w, 1)

            def weighted_hi(s):
                act.wait_ge(s_wh, s + 1)
                act.activation(parts1[:, s * BBLK:(s + 1) * BBLK, 0:F + 1], h_stage(s), ACT.Copy).then_inc(s_hi1, 1)

            def step(g, g0, k):
                t = GROUP * g + k
                band = bands_of(g0) - 1 if k == 1 and g0 in firsts else None
                if on(t, 3):
                    act.wait_ge(s_stats, t - 2)
                    act.activation(std[:, 0:1], mean_var[:, 0, 1:2], ACT.Sqrt, bias=eps[:, :]).then_inc(s_std, 1)
                if band is not None:
                    weights(band)
                if on(t, 0):
                    convert(g, k, 0)
                if on(t, 2):
                    act.wait_ge(s_catT, t - 1)
                    wait(act, s_y, t - 3)
                    act.activation(catT[:, k % 2, :], ps_catT[:, 0:2 * P], ACT.Copy).then_inc(s_catTc, 1)
                if on(t, 4):
                    act.wait_ge(s_x1T, t - 3)
                    wait(act, s_h, t - 5)
                    act.activation(x1T[:, k % 2, :], ps_x1T[:, 0:P], ACT.Copy).then_inc(s_x1Tc, 1)
                    act.dma_start(x1_tiles[t - 4], x1_row[:, k, :]).then_inc(s_x1st[k], 16)
                if band is not None:
                    weighted_hi(band)
                if on(t, 0):
                    convert(g, k, 1)
                if on(t, 4):
                    act.wait_ge(s_h, t - 3)
                    wait(act, s_e, t - 7)
                    wait(act, s_hst[k], 16 * (g - 1))
                    act.activation(h_row[:, k, :], ps_h[:, 0:HCOLS], ACT.Copy).then_inc(s_hc, 1)
                    act.wait_ge(s_hc, t - 3)
                    act.dma_start(h_tiles[t - 4], h_row[:, k, :]).then_inc(s_hst[k], 16)

            def group(g, g0):
                for k in range(GROUP):
                    step(g, g0, k)

            groups_loop(act, group, {0, 1} | firsts)
            group(GROUPS, GROUPS)
            weights(BANDS - 1)
            weighted_hi(BANDS - 1)

            act.wait_ge(s_flag, 1)
            general = act.value_load(flag[0:1, 0:1], min_val=0, max_val=1)
            with act.If(general == 0):
                def store_rows(g, k):
                    act.wait_ge(s_out, GROUP * g + k + 1)
                    act.dma_start(out_tiles[GROUP * g + k], y_out[:, k, :]).then_inc(s_outst[k], 16)

                def group(g):
                    for k in range(GROUP):
                        t = GROUP * g + k
                        act.wait_ge(s_sum1, t + 1)
                        wait(act, s_sum1r, t)
                        act.activation(agg_lo[:, 0:F + 1], ps_agg[k % 2][:, LO:LO + F + 1], ACT.Copy).then_inc(s_lo1c, 1)
                        act.wait_ge(s_st1, t + 1)
                        wait(act, s_rstd1, t - 1)
                        act.activation(std[:, k % 2:k % 2 + 1], mean_var[:, k % 2, 1:2], ACT.Sqrt, bias=eps[:, :])\
                            .then_inc(s_std1, 1)
                        if k > 0:
                            store_rows(g, k - 1)
                        elif not isinstance(g, int):
                            store_rows(g - 1, GROUP - 1)

                group(0)
                with act.Fori(1, GROUPS) as g:
                    group(g)
                store_rows(GROUPS - 1, GROUP - 1)
                for s in range(4):
                    act.wait_ge(s_outst[s], 16 * TILES // 4)
            with act.Else():
                def step(layer, t):
                    u = TILES * layer + t
                    if layer == 1:
                        act.wait_ge(g_masked, t + 1)
                        act.activation(g_rows, g_rows, ACT.Exp, bias=shift[:, :]).then_inc(g_exp, 1)
                    for c in range(NBLK // 4):
                        act.wait_ge(g_T, NBLK // 4 * u + c + 1)
                        wait(act, g_used, NBLK // 4 * u + c - 1)
                        act.activation(g_blockT[:, c % 2, :], g_banks[c % 2][:, :], ACT.Copy).then_inc(g_Tc, 1)
                    if layer == 0:
                        act.wait_ge(g_catT, t + 1)
                        act.activation(catT[:, 0, :], ps_catT[:, 0:2 * P], ACT.Copy).then_inc(g_catTc, 1)
                    act.wait_ge(g_stats, u + 1)
                    act.activation(std[:, 0:1], mean_var[:, 0, 1:2], ACT.Sqrt, bias=eps[:, :]).then_inc(g_std, 1)
                    if layer == 0:
                        act.wait_ge(g_x1T, t + 1)
                        act.activation(x1T[:, 0, :], ps_x1T[:, 0:P], ACT.Copy).then_inc(g_x1Tc, 1)
                        act.wait_ge(g_h, t + 1)
                        wait(act, g_hst, 48 * t)
                        act.activation(h_row[:, 0, :], ps_h[:, 0:HCOLS], ACT.Copy).then_inc(g_hc, 1)

                general_loop(act, step)

        @block.tensor
        def _(pe):
            pe.wait_ge(s_fill, 1)
            pe.wait_ge(s_const, 16 * 4)
            pe.transpose(ps_small[:, 0:P], w1_sb[:, :], ident[:, :])
            pe.matmul(ps_small[:, F:F + 1], w1_sb[:, :], a2_sb[:, :], start=True, stop=True).then_inc(s_w1T, 1)
            pe.wait_ge(s_lo0, 4)
            pe.wait_ge(s_w1Tc, 1)

            def group(g, g0):
                for k in range(GROUP):
                    step(g, g0, k)

            def step(g, g0, k):
                t = GROUP * g + k
                if on(t, 0):
                    wait_apart(pe, (s_trh, 2 * t + 2), (s_aggr, t - 1))
                    contract(pe, ps_agg[k % 2], k % 2, parts0[:, :, 0:2 * F + 1], range(0, NBLK // 2), 0, NBLK - 1)
                if on(t, 1):
                    pe.wait_ge(s_aggr, t)
                    pe.wait_ge(s_xrow[(k - 1) % 4], 16 * (g + (k - 1) // 4 + 1))
                    wait(pe, s_catTc, t - 1)
                    pe.transpose(ps_catT[:, 0:P], agg[:, (k - 1) % 2, :], ident[:, :])
                    pe.transpose(ps_catT[:, P:2 * P], x_row[:, (k - 1) % 4, :], ident[:, :]).then_inc(s_catT, 1)
                if on(t, 3):
                    pe.wait_ge(s_x1, t - 2)
                    wait(pe, s_x1Tc, t - 3)
                    pe.transpose(ps_x1T[:, 0:P], x1_row[:, (k - 3) % 4, :], ident[:, :]).then_inc(s_x1T, 1)
                if on(t, 0):
                    contract(pe, ps_agg[k % 2], k % 2, parts0[:, :, 0:2 * F + 1], range(NBLK // 2, NBLK), 0, NBLK - 1).then_inc(s_agg, 1)
                if isinstance(g, int) and g == SHIFT_GROUP and k == 1:
                    pe.wait_ge(s_max0, 1)
                    pe.transpose(ps_small[0:1, 0:P], gate[:, 0:1], ident[:, :]).then_inc(s_max0T, 1)
                if isinstance(g, int) and g == SHIFT_GROUP and k == 2:
                    pe.wait_ge(s_neg, 1)
                    pe.matmul(ps_small[:, 0:1], ones[0:1, :], verdict[0:1, 2:3], start=True, stop=True)\
                        .then_inc(s_bc, 1)
                if on(t, 1):
                    pe.wait_ge(s_catTc, t)
                    wait(pe, s_z, t - 1)
                    pe.matmul(ps_y[:, 0:F], catT[:, (k - 1) % 2, 0:P], w0_sb[:, 0, :], start=True, stop=False)
                    pe.matmul(ps_y[:, 0:F], catT[:, (k - 1) % 2, P:2 * P], w0_sb[:, 1, :],
                              start=False, stop=True).then_inc(s_y, 1)
                if on(t, 3):
                    pe.wait_ge(s_x1Tc, t - 2)
                    wait(pe, s_hc, t - 3)
                    pe.matmul(ps_h[:, 0:HCOLS], x1T[:, (k - 3) % 2, :], w1T[:, 0:HCOLS],
                              start=True, stop=True).then_inc(s_h, 1)
                if early(g, g0, k, 0):
                    bands = bands_of(g0)
                    wait_apart(pe, (s_lo1, bands), (s_partk, t - EARLY))
                    contract(pe, ps_part, k % 2, parts1, range(0, bands * BBLK), 0, bands * BBLK - 1)\
                        .then_inc(s_part, 1)

            groups_loop(pe, group, {0, SHIFT_GROUP} | {EARLY // GROUP})
            group(GROUPS, GROUPS)

            for t in range(2):
                pe.wait_ge(s_unp, t + 1)
                contract(pe, ps_agg[t], t, parts1, range(0, NBLK - BBLK), 0, NBLK - 1).then_inc(s_head, 1)
                if t == 0:
                    pe.wait_ge(s_gate, 1)
                    for c in range(3):
                        last = pe.transpose(ps_small[0:1, c * P:(c + 1) * P], gate[:, c:c + 1], ident[:, :])
                    last.then_inc(s_redT, 1)

            pe.wait_ge(s_flag, 1)
            general = pe.value_load(flag[0:1, 0:1], min_val=0, max_val=1)
            with pe.If(general == 0):
                pe.wait_ge(s_lo1, BANDS)
                for t in range(2):
                    contract(pe, ps_agg[t], t, parts1, range(NBLK - BBLK, NBLK), 0, NBLK - 1).then_inc(s_sum1, 1)

                def group(g, g0):
                    for k in range(GROUP):
                        t = GROUP * g + k
                        if isinstance(t, int) and t < 2:
                            continue
                        wait_apart(pe, (s_unp, t + 1), (s_sum1r, t - 1))
                        first = bands_of(g0) * BBLK
                        contract(pe, ps_agg[k % 2], k % 2, parts1, range(first, NBLK), first, NBLK - 1)\
                            .then_inc(s_sum1, 1)

                groups_loop(pe, group, {0})
            with pe.Else():
                pe.wait_ge(s_lo1, BANDS)
                for t in range(2):
                    contract(pe, ps_agg[t], t, parts1, [NBLK - 1], 0, NBLK - 1).then_inc(s_head, 1)

                def step(layer, t):
                    u = TILES * layer + t
                    pe.wait_ge(g_made, u + 1)
                    if isinstance(t, int):
                        pe.wait_ge(g_matl, 16 * (1 + 2 * layer))
                        pe.wait_ge(g_ones, 1)

                    def blocks_product(c):
                        pe.wait_ge(g_Tc, NBLK // 4 * u + c + 1)
                        for b in range(4):
                            n = 4 * c + b
                            last = pe.matmul(ps_agg[0][:, 0:HCOLS], g_blockT[:, c % 2, b * P:(b + 1) * P],
                                             g_mat[:, n, :], start=(n == 0), stop=(n == NBLK - 1))
                        last.then_inc(g_used, 1)

                    for c in range(NBLK // 4):
                        wait(pe, g_Tc, NBLK // 4 * u + c - 1)
                        for b in range(4):
                            n = 4 * c + b
                            last = pe.transpose(g_banks[c % 2][:, b * P:(b + 1) * P], g_rows[:, n * P:(n + 1) * P],
                                                ident[:, :])
                        last.then_inc(g_T, 1)
                        if c > 0:
                            blocks_product(c - 1)
                    blocks_product(NBLK // 4 - 1)
                    if layer == 0:
                        pe.wait_ge(g_agg, t + 1)
                        pe.wait_ge(g_xrow, 16 * (t + 1))
                        pe.transpose(ps_catT[:, 0:P], agg[:, 0, :], ident[:, :])
                        pe.transpose(ps_catT[:, P:2 * P], x_row[:, 0, :], ident[:, :]).then_inc(g_catT, 1)
                        pe.wait_ge(g_catTc, t + 1)
                        pe.matmul(ps_y[:, 0:F], catT[:, 0, 0:P], w0_sb[:, 0, :], start=True, stop=False)
                        pe.matmul(ps_y[:, 0:F], catT[:, 0, P:2 * P], w0_sb[:, 1, :],
                                  start=False, stop=True).then_inc(g_y, 1)
                        pe.wait_ge(g_x1, t + 1)
                        pe.transpose(ps_x1T[:, 0:P], x1_row[:, 0, :], ident[:, :]).then_inc(g_x1T, 1)
                        pe.wait_ge(g_x1Tc, t + 1)
                        pe.matmul(ps_h[:, 0:HCOLS], x1T[:, 0, :], w1T[:, 0:HCOLS], start=True, stop=True)\
                            .then_inc(g_h, 1)

                general_loop(pe, step)

        @block.vector
        def _(dve):
            dve.memset(stray[:, :], 0).then_inc(s_stray0, 1)
            for q in range(4):
                blk = slice(q * NBLK // 4, (q + 1) * NBLK // 4)
                dve.wait_ge(s_hi0, q + 1)
                dve.scalar_tensor_tensor(parts0[:, blk, LO:LO + F], x_stage[:, blk, :], XSCALE, parts0[:, blk, 0:F],
                                         ALU.mult, ALU.subtract).then_inc(s_lo0, 1)
            dve.wait_ge(s_const, 16 * 4)
            dve.tensor_tensor(z[:, 0, :], w1_sb[:, :], w1_sb[:, :], ALU.mult).then_inc(s_gate0, 1)
            dve.wait_ge(s_gate0, 1)
            dve.tensor_reduce(gate[:, 6:7], z[:, 0, :], AX.X, ALU.add).then_inc(s_gate0, 1)
            dve.wait_ge(s_fill, 1)
            def transpose_half(g, k, half):
                t = GROUP * g + k
                dve.wait_ge(s_conv, 2 * t + half + 1)
                wait(dve, s_agg, t - 1)
                src = edges[:, half, :, :].bitcast(u32).rearrange("p r (b w) -> p r b w", b=NB)
                dst = edgesT[:, k % 2, :].rearrange("p (b r i) -> p r b i", b=NB, r=NQ)
                dve.transpose(dst[:, 2 * half], src[:, 0])
                dve.transpose(dst[:, 2 * half + 1], src[:, 1]).then_inc(s_trh, 1)

            def exponents(s):
                dve.wait_ge(s_hload, 16 * NQ * (s + 1))
                dve.wait_ge(s_shift, 1)
                dve.tensor_scalar(h_stage(s)[:, :, F], h_stage(s)[:, :, F], shift[:, :], W_CAP, ALU.add, ALU.min)\
                    .then_inc(s_exponent, 1)

            def weighted(s):
                stage = h_stage(s)
                dve.wait_ge(s_w, s + 1)
                dve.tensor_tensor(stage[:, :, 0:F], stage[:, :, 0:F], stage[:, :, F:F + 1].to_broadcast([P, BBLK, F]),
                                  ALU.mult).then_inc(s_wh, 1)

            def weighted_lo(s):
                dve.wait_ge(s_hi1, s + 1)
                blk = slice(s * BBLK, (s + 1) * BBLK)
                dve.tensor_tensor(parts1[:, blk, LO:LO + F + 1], h_stage(s), parts1[:, blk, 0:F + 1],
                                  ALU.subtract).then_inc(s_lo1, 1)

            def step(g, g0, k):
                t = GROUP * g + k
                band = bands_of(g0) - 1 if k == 0 and g0 in firsts else None
                if on(t, 0):
                    if isinstance(g, int) or bands_of(g0):
                        wait(dve, s_part, t - 1 - EARLY)
                    transpose_half(g, k, 0)
                if on(t, 1):
                    bank, s = ps_agg[(k - 1) % 2], (k - 1) % 2
                    dve.wait_ge(s_agg, t)
                    wait(dve, s_aggr, t - 1)
                    dve.reciprocal(rcount[:, :], bank[:, COUNT:COUNT + 1]).then_inc(s_rdeg, 1)
                    dve.wait_ge(s_rdeg, t)
                    dve.tensor_scalar(agg_lo[:, 0:F], bank[:, LO:LO + F], rcount[:, :], None, ALU.mult).then_inc(s_aglo, 1)
                    dve.wait_ge(s_aglo, t)
                    wait(dve, s_catT, t - 2)
                    dve.scalar_tensor_tensor(agg[:, s, :], bank[:, 0:F], rcount[:, :], agg_lo[:, 0:F],
                                             ALU.mult, ALU.add).then_inc(s_aggr, 1)
                if on(t, 2):
                    dve.wait_ge(s_y, t - 1)
                    dve.wait_ge(s_xb, t - 1)
                    wait(dve, s_x1, t - 2)
                    dve.tensor_tensor(z[:, 0, :], ps_y[:, 0:F], xb[:, k % 2, :], ALU.add).then_inc(s_z, 1)
                    dve.wait_ge(s_z, t - 1)
                    dve.bn_stats(stats[:, :], z[:, 0, :]).then_inc(s_bn, 1)
                    wait_apart(dve, (s_bn, t - 1))
                    dve.bn_aggr(mean_var[:, 0, :], stats[:, :]).then_inc(s_stats, 1)
                if band is not None:
                    exponents(band)
                if on(t, 0):
                    transpose_half(g, k, 1)
                if band is not None:
                    weighted(band)
                if early(g, g0, k, 1):
                    scale = BIT_SCALE[(k - 1) % GROUP]
                    dve.wait_ge(s_part, t - EARLY)
                    wait(dve, s_partk, t - 1 - EARLY)
                    dve.tensor_scalar(part_lo[:, :], ps_part[:, LO:LO + F + 1], scale, None, ALU.mult)\
                        .then_inc(s_partlo, 1)
                    dve.wait_ge(s_partlo, t - EARLY)
                    dve.scalar_tensor_tensor(partial[:, t - 1 - EARLY, :], ps_part[:, 0:F + 1], scale, part_lo[:, :],
                                             ALU.mult, ALU.add).then_inc(s_partk, 1)
                if on(t, 0):
                    dve.wait_ge(s_trh, 2 * t + 2)
                    for part in range(CHECKS):
                        words = edgesT[:, k % 2, part * TW // CHECKS:(part + 1) * TW // CHECKS]
                        wait(dve, s_check, CHECKS * t + part)
                        dve.scalar_tensor_tensor(stray[:, :], words, every_byte(0xFF ^ EDGE[k]), stray[:, :],
                                                 ALU.bitwise_and, ALU.bitwise_or).then_inc(s_check, 1)
                    words = slice(bands_of(g0) * BW, TW)
                    bits = edgesT[:, k % 2:k % 2 + 1, words]
                    word = packed[:, bass.ds(g % 2, 1), words]
                    wait(dve, s_pack, t)
                    if k == 0:
                        wait(dve, s_pkst, 16 * (g - 1))
                        dve.tensor_single_scalar(word, bits, every_byte(BIT[k]), ALU.bitwise_and).then_inc(s_pack, 1)
                    else:
                        dve.scalar_tensor_tensor(word, bits, every_byte(BIT[k]), word, ALU.bitwise_and,
                                                 ALU.bitwise_or).then_inc(s_pack, 1)
                if on(t, 2):
                    dve.wait_ge(s_std, t - 1)
                    dve.reciprocal(rstd[:, :], std[:, 0:1]).then_inc(s_rstd, 1)
                    dve.wait_ge(s_rstd, t - 1)
                    wait(dve, s_x1st[(k - 2) % 4], 16 * (g + (k - 2) // 4))
                    dve.tensor_scalar(x1_row[:, (k - 2) % 4, :], z[:, 0, :], mean_var[:, 0, 0:1], rstd[:, :],
                                      ALU.subtract, ALU.mult).then_inc(s_x1, 1)
                if band is not None:
                    weighted_lo(band)
                if isinstance(g, int) and g == 1:
                    blk = slice(k * NBLK // GROUP, (k + 1) * NBLK // GROUP)
                    dve.tensor_reduce(x_big[:, blk], x_stage[:, blk, :], AX.X, ALU.max, apply_absolute_value=True)\
                        .then_inc(s_gate0, 1)
                if isinstance(g, int) and g == SHIFT_GROUP and k == 1:
                    dve.wait_ge(s_e, BTILES)
                    dve.tensor_reduce(gate[:, 0:1], e_all[:, 0:BTILES], AX.X, ALU.max).then_inc(s_max0, 1)
                if isinstance(g, int) and g == SHIFT_GROUP and k == 2:
                    dve.wait_ge(s_max0T, 1)
                    dve.tensor_reduce(top[0:1, 3:4], ps_small[0:1, 0:P], AX.X, ALU.max).then_inc(s_top0, 1)
                    dve.wait_ge(s_top0, 1)
                    dve.tensor_scalar(verdict[0:1, 2:3], top[0:1, 3:4], -1.0, W_SHIFT, ALU.mult, ALU.add)\
                        .then_inc(s_neg, 1)
                if isinstance(g, int) and g == SHIFT_GROUP and k == 3:
                    dve.wait_ge(s_bc, 1)
                    dve.tensor_copy(shift[:, :], ps_small[:, 0:1]).then_inc(s_shift, 1)

            def group(g, g0):
                for k in range(GROUP):
                    step(g, g0, k)

            groups_loop(dve, group, {0, 1, SHIFT_GROUP} | firsts)
            for k in range(2):
                step(GROUPS, GROUPS, k)

            def unpack(g, m, g0, k):
                t = GROUP * g + GROUP * m + k
                words = slice(bands_of(g0) * BW, TW)
                if k == 0:
                    dve.wait_ge(s_pkld[m], 16 * (g + 2))
                wait(dve, s_sum1, t - 1)
                dve.tensor_single_scalar(edgesT[:, k % 2, words], packed_in[:, m, words], every_byte(BIT[k]),
                                         ALU.bitwise_and).then_inc(s_unp, 1)

            dve.wait_ge(s_pack, TILES)
            dve.wait_ge(s_check, CHECKS * TILES)
            dve.wait_ge(s_partk, TILES - EARLY)
            for k in range(2):
                unpack(0, 0, 0, k)

            dve.wait_ge(s_gate0, 2 + GROUP)
            dve.tensor_reduce(gate[:, 4:5], x_big[:, :], AX.X, ALU.max)
            dve.tensor_reduce(gate[:, 5:6], x_big[:, :], AX.X, ALU.min)
            dve.tensor_reduce(gate[:, 3:4], stray[:, :].bitcast(i32), AX.X, ALU.max,
                              apply_absolute_value=True).then_inc(s_gate0, 1)
            dve.wait_ge(s_gate0, 3 + GROUP)
            dve.tensor_single_scalar(okay[:, 0:1], gate[:, 4:5], X_MAX, ALU.is_le)
            dve.tensor_single_scalar(okay[:, 1:2], gate[:, 5:6], X_MIN, ALU.is_ge)
            dve.tensor_single_scalar(okay[:, 2:3], gate[:, 6:7], W_NORM2, ALU.is_le)
            dve.tensor_single_scalar(okay[:, 3:4], gate[:, 3:4], 0.0, ALU.is_equal).then_inc(s_gate0, 1)
            dve.wait_ge(s_gate0, 4 + GROUP)
            dve.tensor_reduce(gate[:, 2:3], okay[:, :], AX.X, ALU.min, negate=True)

            dve.wait_ge(s_e, TILES)
            dve.tensor_reduce(gate[:, 0:1], e_all[:, :], AX.X, ALU.max)
            dve.tensor_reduce(gate[:, 1:2], e_all[:, :], AX.X, ALU.min, negate=True).then_inc(s_gate, 1)
            dve.wait_ge(s_redT, 1)
            dve.tensor_reduce(top[0:1, 0:3], ps_small[0:1, 0:3 * P].rearrange("o (c p) -> o c p", p=P), AX.X,
                              ALU.max).then_inc(s_top, 1)
            dve.wait_ge(s_top, 1)
            dve.tensor_scalar(verdict[0:1, 0:1], top[0:1, 0:1], top[0:1, 3:4], E_ABOVE, ALU.subtract, ALU.is_le)
            dve.tensor_scalar(verdict[0:1, 1:2], top[0:1, 1:2], top[0:1, 3:4], E_BELOW, ALU.add, ALU.is_le)\
                .then_inc(s_vord, 1)
            dve.wait_ge(s_vord, 1)
            dve.tensor_scalar(verdict[0:1, 3:4], verdict[0:1, 0:1], verdict[0:1, 1:2], top[0:1, 2:3], ALU.mult, ALU.mult)\
                .then_inc(s_vord, 1)
            dve.wait_ge(s_vord, 2)
            dve.tensor_scalar(flag[0:1, :], verdict[0:1, 3:4], 1.0, None, ALU.add).then_inc(s_flag, 1)

            exponents(BANDS - 1)
            weighted(BANDS - 1)
            weighted_lo(BANDS - 1)

            general = dve.value_load(flag[0:1, 0:1], min_val=0, max_val=1)
            with dve.If(general == 0):
                def rows_sum(g, g0, j):
                    t, s = GROUP * g + j, j % 2
                    dve.wait_ge(s_lo1c, t + 1)
                    wait(dve, s_z1, t)
                    dve.tensor_tensor(zsum[:, :], ps_agg[s][:, 0:F + 1], agg_lo[:, 0:F + 1], ALU.add)\
                        .then_inc(s_sum1r, 1)
                    dve.wait_ge(s_sum1r, t + 1)
                    if bands_of(g0) if not isinstance(g, int) else t >= EARLY:
                        dve.tensor_tensor(zsum[:, :], zsum[:, :], partial[:, t - EARLY, :], ALU.add).then_inc(s_padd, 1)
                        dve.wait_ge(s_padd, t - EARLY + 1)
                    dve.reciprocal(rcount[:, :], zsum[:, COUNT:COUNT + 1]).then_inc(s_rden, 1)
                    dve.wait_ge(s_rden, t + 1)
                    wait(dve, s_out, t - 1)
                    dve.scalar_tensor_tensor(z1[:, s, :], zsum[:, 0:F], rcount[:, :],
                                             x1_in[:, j // GROUP % 2, j % GROUP, :], ALU.mult, ALU.add).then_inc(s_z1, 1)
                    dve.wait_ge(s_z1, t + 1)
                    wait(dve, s_st1, t)
                    dve.bn_stats(stats[:, :], z1[:, s, :]).then_inc(s_bn1, 1)
                    wait_apart(dve, (s_bn1, t + 1))
                    dve.bn_aggr(mean_var[:, s, :], stats[:, :]).then_inc(s_st1, 1)

                def rows_norm(g, j):
                    t, s = GROUP * g + j, j % 2
                    dve.wait_ge(s_std1, t + 1)
                    wait(dve, s_out, t)
                    dve.reciprocal(rstd[:, :], std[:, s:s + 1]).then_inc(s_rstd1, 1)
                    dve.wait_ge(s_rstd1, t + 1)
                    wait(dve, s_outst[j % 4], 16 * (g + j // 4))
                    dve.tensor_scalar(y_out[:, j % 4, :], z1[:, s, :], mean_var[:, s, 0:1], rstd[:, :],
                                      ALU.subtract, ALU.mult).then_inc(s_out, 1)

                def pair(g, g0):
                    for j in range(2 * GROUP):
                        t = GROUP * g + j
                        if not isinstance(t, int) or t >= 2:
                            unpack(g, j // GROUP, g0, j % GROUP)
                        if on(t, 1):
                            rows_sum(g, g0, j - 1)
                        if on(t, 2):
                            rows_norm(g, j - 2)

                groups_loop(dve, pair, {0, EARLY // GROUP}, per=2)
                rows_sum(GROUPS, GROUPS, -1)
                rows_norm(GROUPS, -2)
                rows_norm(GROUPS, -1)

            with dve.Else():
                def step(layer, t):
                    u = TILES * layer + t
                    steps = 5 if layer == 0 else 7
                    n = [0]

                    def link(ins):
                        n[0] += 1
                        ins.then_inc(g_chain[layer], 1)
                        wait_apart(dve, (g_chain[layer], steps * t + n[0]))

                    dve.wait_ge(g_landed, 16 * (u + 1))
                    g_before(dve, layer, t)
                    if layer == 0:
                        if isinstance(t, int):
                            dve.wait_ge(s_lo1, BANDS)
                        dve.tensor_copy(g_rows, g_adj).then_inc(g_made, 1)
                    else:
                        if isinstance(t, int):
                            dve.wait_ge(g_matl, 16 * 3)
                        link(dve.tensor_scalar(g_rows, g_adj, 0.0, -1e38, ALU.is_equal, ALU.mult))
                        link(dve.tensor_tensor(g_rows, g_rows, g_e, ALU.add))
                        link(dve.tensor_reduce(top_row[:, :], g_rows, AX.X, ALU.max))
                        dve.tensor_scalar(shift[:, :], top_row[:, :], -1.0, None, ALU.mult).then_inc(g_masked, 1)
                        dve.wait_ge(g_exp, t + 1)
                        dve.scalar_tensor_tensor(g_rows, g_adj, 0.0, g_rows, ALU.not_equal, ALU.mult)\
                            .then_inc(g_made, 1)
                    dve.wait_ge(g_used, NBLK // 4 * (u + 1))
                    dve.wait_ge(g_xrow, 16 * (u + 1))
                    link(dve.reciprocal(rcount[:, :], ps_agg[0][:, COUNT:COUNT + 1]))
                    if layer == 0:
                        dve.tensor_scalar(agg[:, 0, :], ps_agg[0][:, 0:F], rcount[:, :], None, ALU.mult).then_inc(g_agg, 1)
                        dve.wait_ge(g_y, t + 1)
                        link(dve.tensor_tensor(z[:, 0, :], ps_y[:, 0:F], bias[:, :], ALU.add))
                        link(dve.tensor_tensor(z[:, 0, :], z[:, 0, :], x_row[:, 0, :], ALU.add))
                    else:
                        link(dve.scalar_tensor_tensor(z[:, 0, :], ps_agg[0][:, 0:F], rcount[:, :], x_row[:, 0, :],
                                                      ALU.mult, ALU.add))
                    link(dve.bn_stats(stats[:, :], z[:, 0, :]))
                    dve.bn_aggr(mean_var[:, 0, :], stats[:, :]).then_inc(g_stats, 1)
                    dve.wait_ge(g_std, u + 1)
                    link(dve.reciprocal(rstd[:, :], std[:, 0:1]))
                    if layer == 0:
                        wait(dve, g_hst, 48 * t)
                        dve.tensor_scalar(x1_row[:, 0, :], z[:, 0, :], mean_var[:, 0, 0:1], rstd[:, :],
                                          ALU.subtract, ALU.mult).then_inc(g_x1, 1)
                    else:
                        wait(dve, g_outst, 16 * t)
                        dve.tensor_scalar(y_out[:, 0, :], z[:, 0, :], mean_var[:, 0, 0:1], rstd[:, :],
                                          ALU.subtract, ALU.mult).then_inc(g_out, 1)
                    assert n[0] == steps, n[0]

                general_loop(dve, step)

        @block.gpsimd
        def _(pool):
            pool.memset(ident[:, :], 0.0).then_inc(s_id, 1)
            pool.memset(ones[:, :], 1.0)
            pool.memset(eps[:, :], EPS)
            pool.memset(parts0[:, :, COUNT:COUNT + 1], XSCALE)
            pool.wait_ge(s_id, 1)
            pool.affine_select(out=ident[:, :], in_=ident[:, :], compare_op=ALU.not_equal, fill=1.0, base=0,
                               pattern=[[-1, P]], channel_multiplier=1).then_inc(s_fill, 1)
            pool.wait_ge(s_const, 16 * 4)

            def step(g, g0, k):
                t = GROUP * g + k
                if on(t, 4):
                    pool.wait_ge(s_hc, t - 3)
                    pool.tensor_copy(e_all[:, bass.ds(t - 4, 1)], h_row[:, k, F:F + 1]).then_inc(s_e, 1)
                if on(t, 0):
                    pool.wait_ge(s_xrow[k], 16 * (g + 1))
                    wait(pool, s_z, t - 1)
                    pool.tensor_tensor(xb[:, k % 2, :], x_row[:, k, :], bias[:, :], ALU.add).then_inc(s_xb, 1)
                if k == 0 and g0 > 0:
                    store_group(g - 1, g0 - 1)

            def store_group(g, g0):
                words = slice(bands_of(g0) * BW, TW)
                pool.wait_ge(s_pack, GROUP * (g + 1))
                wait(pool, s_pkst, 16 * g)
                pool.dma_start(packed_dram[g][:, words], packed[:, bass.ds(g % 2, 1), words].rearrange("p o w -> p (o w)"))\
                    .then_inc(s_pkst, 16)

            def group(g, g0):
                for k in range(GROUP):
                    step(g, g0, k)

            groups_loop(pool, group, {0, 1} | firsts)
            group(GROUPS, GROUPS)

            pool.wait_ge(s_flag, 1)
            general = pool.value_load(flag[0:1, 0:1], min_val=0, max_val=1)
            with pool.If(general == 0):
                pass
            with pool.Else():
                pool.wait_ge(s_lo1, BANDS)
                pool.wait_ge(s_head, 4)
                pool.memset(g_mat[:, :, F:F + 1], 1.0).then_inc(g_ones, 1)

                def step(layer, t):
                    if layer == 0:
                        pool.wait_ge(g_hc, t + 1)
                        pool.dma_start(h_tiles[t], h_row[:, 0, :]).then_inc(g_hst, 16)
                        pool.dma_start(e_tiles[t], h_row[:, 0, F:F + 1]).then_inc(g_hst, 16)
                        pool.dma_start(x1_tiles[t], x1_row[:, 0, :]).then_inc(g_hst, 16)
                    else:
                        pool.wait_ge(g_out, t + 1)
                        pool.dma_start(out_tiles[t], y_out[:, 0, :]).then_inc(g_outst, 16)

                general_loop(pool, step)
                pool.wait_ge(g_outst, 16 * TILES)


_INS = ['x', 'adj', 'L0_gnn_weight', 'L0_gnn_bias', 'L1_gnn_W', 'L1_gnn_a']


def kernel(**inputs):
    import numpy as _np
    import concourse.bacc as _bacc
    from concourse import mybir as _mybir
    from concourse.bass_utils import run_bass_kernel_spmd as _run

    nc = _bacc.Bacc("TRN2", target_bir_lowering=False, num_devices=1)
    arrays, args = {}, []
    for name in _INS:
        a = _np.ascontiguousarray(inputs[name])
        arrays[f"in_{name}_dram"] = a
        args.append(nc.dram_tensor(f"in_{name}_dram", a.shape, _mybir.dt.from_np(a.dtype), kind="ExternalInput").ap())
    out_shape = inputs['x'].shape
    args.append(nc.dram_tensor("out_0_dram", out_shape, _mybir.dt.float32, kind="ExternalOutput").ap())
    bass_two_graph_layers(nc, *args)
    r = _run(nc, [arrays], core_ids=[0])
    return r.results[0]["out_0_dram"]
```

```python
import math
from contextlib import ExitStack

import concourse.bass as bass
from concourse import mybir


def bass_two_graph_layers(
    nc: bass.Bass,
    x: bass.AP,
    adj: bass.AP,
    w0: bass.AP,
    b0: bass.AP,
    w1: bass.AP,
    a1: bass.AP,
    out: bass.AP,
):
    fp32, fp16, fp8 = mybir.dt.float32, mybir.dt.float16, mybir.dt.float8e4
    i32, u32 = mybir.dt.int32, mybir.dt.uint32
    ALU, ACT, AX = mybir.AluOpType, mybir.ActivationFunctionType, mybir.AxisListType

    N, F = x.shape
    P = 128
    QUAD = 32
    NQ = P // QUAD
    BYTES = 4
    BANDS = 4
    JB = N // BANDS
    JQ = N // NQ
    NB = JQ // (QUAD * BYTES)
    NBLK = NB * BYTES
    BBLK = NBLK // BANDS
    TILES = N // P
    BTILES = TILES // BANDS
    GROUP = 4
    GROUPS = TILES // GROUP
    TW = NB * P
    BW = TW // BANDS
    SLOTS = 4
    PIECES = 4
    CHECKS = 4
    HCOLS = F + 1
    XCOLS = 2 * F + 2
    LO = F + 1
    COUNT = F
    DELAY = 8
    EARLY = BTILES + DELAY
    SHIFT_GROUP = BTILES // GROUP + 1

    LATE = EARLY - BTILES
    BANDS_LATE = 2

    def bands_of(g):
        return max(0, (GROUP * g - DELAY) // BTILES)

    def bands_done(g):
        return BANDS_LATE if LATE <= GROUP * g < EARLY else bands_of(g)

    XSCALE = 4096.0
    X_MAX, X_MIN = 15.0, 2.0 ** -14
    W_SHIFT = 8.0 * math.log(2.0)
    E_ABOVE = 3.0 * math.log(2.0)
    W_CAP = W_SHIFT + E_ABOVE + 0.01
    E_BELOW = 7.0
    W_NORM2 = 7.0
    EPS = 1e-5
    EDGE = [0x38, 0x38, 0x38, 0x40]
    BIT = [0x08, 0x10, 0x20, 0x40]
    BIT_SCALE = [2.0 ** -6, 2.0 ** -5, 2.0 ** -3, 1.0]

    def every_byte(b):
        return b * 0x01010101

    packed_dram = nc.dram_tensor("packed_adj", (GROUPS, P, TW), u32, kind="Internal").ap()
    h_dram = nc.dram_tensor("h_rows", (N, HCOLS), fp32, kind="Internal").ap()
    part_dram = nc.dram_tensor("partial_sums", (N, HCOLS), fp32, kind="Internal").ap()
    x1_dram = nc.dram_tensor("x1_rows", (N, F), fp32, kind="Internal").ap()
    e_dram = nc.dram_tensor("e_row", (TILES, P), fp32, kind="Internal").ap()

    x_bands = x.rearrange("(s a b p c) f -> s a p b (c f)", s=BANDS, a=NQ, p=QUAD, c=BYTES)
    h_bands = h_dram.rearrange("(s a b p c) f -> s a p b (c f)", s=BANDS, a=NQ, p=QUAD, c=BYTES)
    adj_halves = adj.rearrange("(n g q) (s a j) -> n a g q s j", g=2, q=QUAD, s=BANDS, a=NQ)
    adj_tiles = adj.rearrange("(t p) j -> t p j", p=P)
    x_tiles = x.rearrange("(t p) f -> t p f", p=P)
    h_tiles = h_dram.rearrange("(t p) f -> t p f", p=P)
    part_tiles = part_dram.rearrange("(t p) f -> t p f", p=P)
    part_groups = part_dram.rearrange("(g k p) f -> g p k f", k=GROUP, p=P)
    x1_tiles = x1_dram.rearrange("(t p) f -> t p f", p=P)
    x1_groups = x1_dram.rearrange("(g k p) f -> g p k f", k=GROUP, p=P)
    e_tiles = e_dram.rearrange("t (p o) -> t p o", o=1)
    e_row = e_dram.rearrange("(o t) p -> o (t p)", o=1)
    out_tiles = out.rearrange("(t p) f -> t p f", p=P)

    ctx = ExitStack()
    with ctx:
        def sb(name, shape, dt):
            return ctx.enter_context(nc.sbuf_tensor(name, shape, dt))

        def ps(name):
            return ctx.enter_context(nc.psum_tensor(name, [P, 512], fp32))

        def sem(name):
            return ctx.enter_context(nc.semaphore(name))

        adj_in = sb("adj_in", [P, SLOTS, 2, JQ], i32)
        edges = sb("edges", [P, 2, 2, JQ], fp8)
        edgesT = sb("edgesT", [P, 2, TW], u32)
        packed = sb("packed", [P, 2, TW], u32)
        parts0 = sb("parts0", [P, NBLK, XCOLS], fp16)
        parts1 = sb("parts1", [P, NBLK, XCOLS], fp16)
        partial = sb("partial", [P, 4, HCOLS], fp32)
        late = sb("late", [P, BTILES, HCOLS], fp32)
        late_words = sb("late_words", [P, 2, BW], u32)
        lateT = sb("lateT", [P, 2, BW], u32)
        late_lo = sb("late_lo", [P, HCOLS], fp32)
        stray = sb("stray", [P, TW // CHECKS], u32)
        x_row = sb("x_row", [P, 4, F], fp32)
        xb = sb("xb", [P, 2, F], fp32)
        agg_lo = sb("agg_lo", [P, F + 1], fp32)
        part_lo = sb("part_lo", [P, F + 1], fp32)
        agg = sb("agg", [P, 2, F], fp32)
        catT = sb("catT", [P, 2, 2 * P], fp32)
        z = sb("z", [P, 1, F], fp32)
        z1 = agg
        zsum = part_lo
        stats = sb("stats", [P, 6], fp32)
        mean_var = sb("mean_var", [P, 2, 2], fp32)
        std = sb("std", [P, 2], fp32)
        rstd = sb("rstd", [P, 1], fp32)
        rcount = sb("rcount", [P, 1], fp32)
        x1_row = sb("x1_row", [P, 4, F], fp32)
        x1T = sb("x1T", [P, 2, P], fp32)
        h_row = sb("h_row", [P, 4, HCOLS], fp32)
        e_all = sb("e_all", [P, TILES], fp32)
        y_out = x1_row
        w0_sb = sb("w0_sb", [P, 2, F], fp32)
        w1_sb = sb("w1_sb", [P, F], fp32)
        w1T = sb("w1T", [P, HCOLS], fp32)
        a2_sb = sb("a2_sb", [P, 1], fp32)
        bias = sb("bias", [P, F], fp32)
        ident = sb("ident", [P, P], fp32)
        ones = sb("ones", [1, P], fp32)
        eps = sb("eps", [P, 1], fp32)
        x_big = sb("x_big", [P, NBLK], fp32)
        gate = sb("gate", [P, 8], fp32)
        okay = sb("okay", [P, 4], fp32)
        top = sb("top", [1, 4], fp32)
        verdict = sb("verdict", [1, 4], fp32)
        flag = sb("flag", [1, 1], i32)
        shift = sb("shift", [P, 1], fp32)
        top_row = sb("top_row", [P, 1], fp32)

        x_stage = parts1[:, :, :].rearrange("p n f -> p (n f)").bitcast(fp32)[:, 0:NBLK * F]\
            .rearrange("p (n f) -> p n f", f=F)
        adj_flat = adj_in[:, :, :, :].rearrange("p s g j -> p (s g j)")
        packed_in = adj_flat[:, 0:2 * TW].bitcast(u32).rearrange("p (s w) -> p s w", s=2)
        x1_in = adj_flat[:, 2 * TW:2 * TW + 2 * GROUP * F].bitcast(fp32)\
            .rearrange("p (s k f) -> p s k f", s=2, k=GROUP)

        part_in = adj_flat[:, 5 * TW:5 * TW + 2 * GROUP * HCOLS].bitcast(fp32)\
            .rearrange("p (s k f) -> p s k f", s=2, k=GROUP)

        def h_stage(s):
            if s < BANDS - 1:
                mem = parts1[:, (s + 1) * BBLK:(s + 2) * BBLK, :].rearrange("p n f -> p (n f)").bitcast(fp32)
            else:
                mem = adj_flat[:, 3 * TW:3 * TW + BBLK * HCOLS].bitcast(fp32)
            return mem.rearrange("p (n f) -> p n f", f=HCOLS)

        g_adj = adj_flat[:, 0:N]
        g_rows = adj_flat[:, N:2 * N].bitcast(fp32)
        g_mat = parts1[:, :, :].rearrange("p n f -> p (n f)").bitcast(fp32).rearrange("p (n f) -> p n f", f=HCOLS)
        g_e = parts0[:, :, :].rearrange("p n f -> p (n f)").bitcast(fp32)[:, 0:N]
        g_blockT = edgesT[:, 0, 0:8 * P].bitcast(fp32).rearrange("p (s i) -> p s i", s=2)

        ps_agg = [ps("ps_agg0"), ps("ps_agg1")]
        ps_part = ps("ps_part")
        ps_catT = ps("ps_catT")
        ps_y = ps("ps_y")
        ps_x1T = ps("ps_x1T")
        ps_h = ps("ps_h")
        ps_small = ps("ps_small")
        g_banks = [ps_agg[1], ps_small]

        s_xload = sem("x_landed")
        s_const = sem("weights_landed")
        s_fill = sem("constants_filled")
        s_id = sem("ident_cleared")
        s_w1T = sem("w1T_done")
        s_w1Tc = sem("w1T_copied")
        s_hi0 = sem("x_hi_made")
        s_lo0 = sem("x_lo_made")
        s_gate0 = sem("gates0_made")
        s_adj = [sem(f"adj_landed{s}") for s in range(SLOTS)]
        s_conv = sem("half_converted")
        s_trh = sem("half_transposed")
        s_check = sem("checked")
        s_pack = sem("tile_packed")
        s_pkst = sem("packed_stored")
        s_agg = sem("agg_summed")
        s_rdeg = sem("rdegree_made")
        s_aglo = sem("agg_lo_scaled")
        s_aggr = sem("agg_made")
        s_part = sem("partial_summed")
        s_partlo = sem("partial_lo_scaled")
        s_partk = sem("partial_made")
        s_partst = [sem(f"partial_stored{s}") for s in range(4)]
        s_lateld = sem("late_words_landed")
        s_lateun = sem("late_unpacked")
        s_late = sem("late_summed")
        s_latelo = sem("late_lo_added")
        s_latek = sem("late_kept")
        s_late0 = sem("late_cleared")
        s_xrow = [sem(f"x_row_landed{s}") for s in range(4)]
        s_xb = sem("x_plus_bias_made")
        s_catT = sem("catT_done")
        s_catTc = sem("catT_copied")
        s_y = sem("y_done")
        s_z = sem("z_made")
        s_bn = sem("bn_made")
        s_stats = sem("stats_made")
        s_std = sem("std_made")
        s_rstd = sem("rstd_made")
        s_x1 = sem("x1_made")
        s_x1st = [sem(f"x1_stored{s}") for s in range(4)]
        s_x1T = sem("x1T_done")
        s_x1Tc = sem("x1T_copied")
        s_h = sem("h_done")
        s_hc = sem("h_copied")
        s_hst = [sem(f"h_stored{s}") for s in range(4)]
        s_e = sem("e_gathered")
        s_max0 = sem("max_made")
        s_max0T = sem("max_transposed")
        s_top0 = sem("band0_max_made")
        s_neg = sem("shift_made")
        s_bc = sem("shift_broadcast")
        s_shift = sem("shift_copied")
        s_hload = sem("h_landed")
        s_exponent = sem("exponents_made")
        s_w = sem("weights_made")
        s_wh = sem("weighted_made")
        s_hi1 = sem("weighted_hi_made")
        s_lo1 = sem("weighted_lo_made")
        s_gate = sem("gates_made")
        s_redT = sem("gates_transposed")
        s_top = sem("extremes_made")
        s_vord = sem("verdict_steps")
        s_flag = sem("flag_made")
        s_pkld = [sem(f"packed_landed{s}") for s in range(2)]
        s_partld = [sem(f"partial_landed{s}") for s in range(2)]
        s_unp = sem("unpacked")
        s_head = sem("first_bands_summed")
        s_sum1 = sem("sum1_done")
        s_lo1c = sem("sum1_lo_copied")
        s_sum1r = sem("sum1_read")
        s_padd = sem("partial_added")
        s_rden = sem("rdenominator_made")
        s_z1 = sem("z1_made")
        s_bn1 = sem("bn1_made")
        s_st1 = sem("stats1_made")
        s_std1 = sem("std1_made")
        s_rstd1 = sem("rstd1_made")
        s_out = sem("out_made")
        s_outst = [sem(f"out_stored{s}") for s in range(4)]
        g_landed = sem("g_adj_landed")
        g_matl = sem("g_matrix_landed")
        g_ones = sem("g_ones_filled")
        g_made = sem("g_rows_made")
        g_masked = sem("g_exponents_masked")
        g_exp = sem("g_exp_made")
        g_T = sem("g_blocks_transposed")
        g_Tc = sem("g_blocks_copied")
        g_used = sem("g_blocks_used")
        g_agg = sem("g_agg_made")
        g_xrow = sem("g_x_row_landed")
        g_catT = sem("g_catT_done")
        g_catTc = sem("g_catT_copied")
        g_y = sem("g_y_done")
        g_stats = sem("g_stats_made")
        g_std = sem("g_std_made")
        g_x1 = sem("g_x1_made")
        g_x1T = sem("g_x1T_done")
        g_x1Tc = sem("g_x1T_copied")
        g_h = sem("g_h_done")
        g_hc = sem("g_h_copied")
        g_hst = sem("g_rows_stored")
        g_out = sem("g_out_made")
        g_outst = sem("g_out_stored")
        g_chain = [sem(f"g_vector_steps{layer}") for layer in range(2)]

        block = ctx.enter_context(nc.Block())

        def wait(eng, semaphore, count):
            if not isinstance(count, int) or count > 0:
                eng.wait_ge(semaphore, count)

        def wait_apart(eng, *waits):
            waits = [(semaphore, count if isinstance(count, int) else eng.to_reg(count)) for semaphore, count in waits]
            eng.wait_ge(s_fill, 1)
            for semaphore, count in waits:
                wait(eng, semaphore, count)

        def on(t, lag):
            return not isinstance(t, int) or 0 <= t - lag < TILES

        def groups_loop(eng, body, single, per=1, bands=bands_of):
            g = 0
            while g < GROUPS:
                end = g + per
                while end < GROUPS and g not in single and end not in single and bands(end) == bands(g):
                    end += per
                if end == g + per:
                    body(g, g)
                else:
                    with eng.Fori(g // per, end // per) as r:
                        body(r * per, g)
                g = end

        def early(g, g0, k, lag):
            return bands_of(g0) > 0 if not isinstance(g, int) else EARLY <= GROUP * g + k - lag < TILES

        def making_up(g, g0, k, lag):
            if not isinstance(g, int):
                return 0 < bands_of(g0) <= BANDS_LATE
            return EARLY <= GROUP * g + k - lag < EARLY + BANDS_LATE * BTILES

        def late_index(g, g0, k, lag):
            bands = bands_of(g0) if not isinstance(g, int) else bands_of((GROUP * g + k - lag) // GROUP)
            return GROUP * g + k - lag - EARLY - BTILES * (bands - 1)

        def contract(eng, bank, words, moving, blocks, first, last, base=0):
            rows = words.bitcast(fp8).rearrange("p (b i c) -> p b c i", i=P, c=BYTES)
            cols = moving.shape[2]
            for n in blocks:
                done = eng.matmul(bank[:, 0:cols], rows[:, (n - base) // BYTES, n % BYTES, :], moving[:, n, :],
                                  start=(n == first), stop=(n == last))
            return done

        def general_loop(eng, step):
            for layer in range(2):
                step(layer, 0)
                with eng.Fori(1, TILES) as t:
                    step(layer, t)

        def g_before(eng, layer, t):
            if layer == 0:
                wait(eng, g_hc, t)
            elif isinstance(t, int):
                eng.wait_ge(g_hc, TILES)
            else:
                eng.wait_ge(g_out, t)

        firsts = {g for g in range(1, GROUPS) if bands_of(g) > bands_of(g - 1)}

        @block.sync
        def _(sp):
            for s in range(BANDS):
                for a in range(NQ):
                    sp.dma_start(x_stage[QUAD * a:QUAD * (a + 1), s * BBLK:(s + 1) * BBLK, :]
                                 .rearrange("p (b c) f -> p b (c f)", c=BYTES), x_bands[s, a]).then_inc(s_xload, 16)

            def load_band(s):
                for slot in range(4):
                    sp.wait_ge(s_hst[slot], 16 * BTILES // 4 * (s + 1))
                for a in range(NQ):
                    sp.dma_start(h_stage(s)[QUAD * a:QUAD * (a + 1), :, :].rearrange("p (b c) f -> p b (c f)", c=BYTES),
                                 h_bands[s, a]).then_inc(s_hload, 16)

            def group(g, g0):
                if g0 in firsts:
                    load_band(bands_of(g0) - 1)
                if making_up(g, g0, 0, 0):
                    band = bands_of(g0) - 1
                    source = LATE // GROUP + g - EARLY // GROUP - BTILES // GROUP * band
                    words_from = packed_dram[source][:, band * BW:(band + 1) * BW]
                    words_to = late_words[:, bass.ds(g % 2, 1), :].rearrange("p o w -> p (o w)")
                    counts = [16 * (source + 1), 16 * (g - EARLY // GROUP), GROUP * (g - EARLY // GROUP - 1)]
                    stored, loaded, unpacked = [n if isinstance(n, int) else sp.to_reg(n) for n in counts]
                    sp.wait_ge(s_pkst, stored)
                    wait(sp, s_lateld, loaded)
                    wait(sp, s_lateun, unpacked)
                    sp.dma_start(words_to, words_from).then_inc(s_lateld, 16)
                for k in range(GROUP):
                    t = GROUP * g + k
                    for half in range(2):
                        n = 2 * k + half
                        slot = n % SLOTS
                        wait(sp, s_conv, 2 * GROUP * g + n - SLOTS + 1)
                        for a in range(NQ):
                            for r in range(2):
                                sp.dma_start(adj_in[QUAD * a:QUAD * (a + 1), slot, r, :]
                                             .rearrange("p (s j) -> p s j", s=BANDS),
                                             adj_halves[2 * GROUP * g + n, a, r]).then_inc(s_adj[slot], 16)
                    wait(sp, s_catT, t - 3)
                    wait(sp, s_xb, t - 3)
                    sp.dma_start(x_row[:, k, :], x_tiles[t]).then_inc(s_xrow[k], 16)

            groups_loop(sp, group, {0, EARLY // GROUP + 1} | firsts)

            def load_group(g, s, bands, with_partial):
                sp.dma_start(packed_in[:, s, bands * BW:TW], packed_dram[g][:, bands * BW:TW]).then_inc(s_pkld[s], 16)
                sp.dma_start(x1_in[:, s, :, :], x1_groups[g]).then_inc(s_pkld[s], 16)
                if with_partial:
                    sp.dma_start(part_in[:, s, :, :], part_groups[g]).then_inc(s_partld[s], 16)

            sp.wait_ge(s_conv, 2 * TILES)
            sp.wait_ge(s_pkst, 16 * 2)
            for slot in range(4):
                sp.wait_ge(s_x1st[slot], 16 * 2)
            for s in range(2):
                load_group(s, s, 0, False)
            load_band(BANDS - 1)
            sp.wait_ge(s_pkst, 16 * GROUPS)
            for slot in range(4):
                sp.wait_ge(s_x1st[slot], 16 * TILES // 4)
                sp.wait_ge(s_partst[slot], 16 * (TILES - EARLY) // 4)

            sp.wait_ge(s_flag, 1)
            general = sp.value_load(flag[0:1, 0:1], min_val=0, max_val=1)
            with sp.If(general == 0):
                def store_rows(g):
                    for k in range(GROUP):
                        sp.wait_ge(s_out, GROUP * g + k + 1)
                        sp.dma_start(out_tiles[GROUP * g + k], y_out[:, k, :]).then_inc(s_outst[k], 16)

                def pair(g, g0):
                    if isinstance(g, int) and g == 0:
                        return
                    for s in range(2):
                        sp.wait_ge(s_z1, GROUP * (g + s - 1))
                        load_group(g + s, s, bands_done(g0), GROUP * g0 >= EARLY)
                        store_rows(g + s - 2)

                groups_loop(sp, pair, {0}, per=2, bands=bands_done)
                for g in range(GROUPS - 2, GROUPS):
                    store_rows(g)
                for k in range(GROUP):
                    sp.wait_ge(s_outst[k], 16 * TILES // GROUP)
            with sp.Else():
                def step(layer, t):
                    g_before(sp, layer, t)
                    if isinstance(t, int) and layer == 0:
                        sp.wait_ge(s_lo1, BANDS - 1 + PIECES)
                        sp.wait_ge(s_head, 4)
                        for s in range(2):
                            sp.wait_ge(s_pkld[s], 16 * 2)
                        sp.dma_start(g_mat[:, :, 0:F], x.rearrange("(n p) f -> p n f", p=P)).then_inc(g_matl, 16)
                    if isinstance(t, int) and layer == 1:
                        sp.wait_ge(g_hst, 48 * TILES)
                        sp.dma_start(g_mat[:, :, 0:F], h_dram[:, 0:F].rearrange("(n p) f -> p n f", p=P))\
                            .then_inc(g_matl, 16)
                        sp.dma_start(g_e, e_row.to_broadcast([P, N])).then_inc(g_matl, 16)
                    sp.dma_start(g_adj, adj_tiles[t]).then_inc(g_landed, 16)
                    sp.dma_start(x_row[:, 0, :], (x_tiles if layer == 0 else x1_tiles)[t]).then_inc(g_xrow, 16)

                general_loop(sp, step)

        @block.scalar
        def _(act):
            act.dma_start(w1_sb[:, :], w1).then_inc(s_const, 16)
            act.dma_start(w0_sb[:, :, :], w0.rearrange("(c p) f -> p c f", p=P)).then_inc(s_const, 16)
            act.dma_start(a2_sb[:, :], a1[F:2 * F].rearrange("(p o) -> p o", o=1)).then_inc(s_const, 16)
            act.dma_start(bias[:, :], b0.rearrange("(o f) -> o f", o=1).to_broadcast([P, F])).then_inc(s_const, 16)
            act.wait_ge(s_w1T, 1)
            act.activation(w1T[:, 0:F + 1], ps_small[:, 0:F + 1], ACT.Copy).then_inc(s_w1Tc, 1)
            act.wait_ge(s_fill, 1)
            act.wait_ge(s_xload, 16 * NQ * BANDS)
            for q in range(4):
                blk = slice(q * NBLK // 4, (q + 1) * NBLK // 4)
                act.activation(parts0[:, blk, 0:F], x_stage[:, blk, :], ACT.Copy, scale=XSCALE).then_inc(s_hi0, 1)

            def convert(g, k, half):
                t, n = GROUP * g + k, 2 * k + half
                wait_apart(act, (s_adj[n % SLOTS], 2 * 16 * NQ * (2 * g + n // SLOTS + 1)),
                           (s_trh, 2 * t + half - 1))
                act.activation(edges[:, half, :, :], adj_in[:, n % SLOTS, :, :], ACT.Copy,
                               scale=2.0 if k == GROUP - 1 else 1.0, saturate=False).then_inc(s_conv, 1)

            def weights(s):
                act.wait_ge(s_exponent, s + 1)
                act.activation(h_stage(s)[:, :, F], h_stage(s)[:, :, F], ACT.Exp).then_inc(s_w, 1)

            def weighted_hi(s, piece=0, pieces=1):
                act.wait_ge(s_wh, s + piece + 1)
                stage = h_stage(s)[:, piece * BBLK // pieces:(piece + 1) * BBLK // pieces, :]
                blk = slice(s * BBLK + piece * BBLK // pieces, s * BBLK + (piece + 1) * BBLK // pieces)
                act.activation(parts1[:, blk, 0:F + 1], stage, ACT.Copy).then_inc(s_hi1, 1)

            def step(g, g0, k):
                t = GROUP * g + k
                band = bands_of(g0) - 1 if g0 in firsts else None
                if on(t, 3):
                    act.wait_ge(s_stats, t - 2)
                    act.activation(std[:, 0:1], mean_var[:, 0, 1:2], ACT.Sqrt, bias=eps[:, :]).then_inc(s_std, 1)
                if early(g, g0, k, 3):
                    act.wait_ge(s_partk, t - 2 - EARLY)
                    act.dma_start(part_tiles[t - 3], partial[:, (k - 3) % 4, :]).then_inc(s_partst[(k - 3) % 4], 16)
                if on(t, 0):
                    convert(g, k, 0)
                if band is not None and k == 1:
                    weighted_hi(band)
                if on(t, 2):
                    act.wait_ge(s_catT, t - 1)
                    wait(act, s_y, t - 3)
                    act.activation(catT[:, k % 2, :], ps_catT[:, 0:2 * P], ACT.Copy).then_inc(s_catTc, 1)
                if on(t, 4):
                    act.wait_ge(s_x1T, t - 3)
                    wait(act, s_h, t - 5)
                    act.activation(x1T[:, k % 2, :], ps_x1T[:, 0:P], ACT.Copy).then_inc(s_x1Tc, 1)
                    act.dma_start(x1_tiles[t - 4], x1_row[:, k, :]).then_inc(s_x1st[k], 16)
                if band is not None and k == 0:
                    weights(band)
                if on(t, 0):
                    convert(g, k, 1)
                if on(t, 4):
                    act.wait_ge(s_h, t - 3)
                    wait(act, s_e, t - 7)
                    wait(act, s_hst[k], 16 * (g - 1))
                    act.activation(h_row[:, k, :], ps_h[:, 0:HCOLS], ACT.Copy).then_inc(s_hc, 1)
                    act.wait_ge(s_hc, t - 3)
                    act.dma_start(h_tiles[t - 4], h_row[:, k, :]).then_inc(s_hst[k], 16)

            def group(g, g0):
                for k in range(GROUP):
                    step(g, g0, k)

            groups_loop(act, group, {0, 1} | firsts)
            group(GROUPS, GROUPS)
            weights(BANDS - 1)
            for piece in range(PIECES):
                weighted_hi(BANDS - 1, piece, PIECES)

            act.wait_ge(s_flag, 1)
            general = act.value_load(flag[0:1, 0:1], min_val=0, max_val=1)
            with act.If(general == 0):
                def group(g):
                    for k in range(GROUP):
                        t = GROUP * g + k
                        act.wait_ge(s_sum1, t + 1)
                        wait(act, s_sum1r, t)
                        act.activation(agg_lo[:, 0:F + 1], ps_agg[k % 2][:, LO:LO + F + 1], ACT.Copy).then_inc(s_lo1c, 1)
                        act.wait_ge(s_st1, t + 1)
                        wait(act, s_rstd1, t - 1)
                        act.activation(std[:, k % 2:k % 2 + 1], mean_var[:, k % 2, 1:2], ACT.Sqrt, bias=eps[:, :])\
                            .then_inc(s_std1, 1)

                group(0)
                with act.Fori(1, GROUPS) as g:
                    group(g)
            with act.Else():
                def step(layer, t):
                    u = TILES * layer + t
                    if layer == 1:
                        act.wait_ge(g_masked, t + 1)
                        act.activation(g_rows, g_rows, ACT.Exp, bias=shift[:, :]).then_inc(g_exp, 1)
                    for c in range(NBLK // 4):
                        act.wait_ge(g_T, NBLK // 4 * u + c + 1)
                        wait(act, g_used, NBLK // 4 * u + c - 1)
                        act.activation(g_blockT[:, c % 2, :], g_banks[c % 2][:, :], ACT.Copy).then_inc(g_Tc, 1)
                    if layer == 0:
                        act.wait_ge(g_catT, t + 1)
                        act.activation(catT[:, 0, :], ps_catT[:, 0:2 * P], ACT.Copy).then_inc(g_catTc, 1)
                    act.wait_ge(g_stats, u + 1)
                    act.activation(std[:, 0:1], mean_var[:, 0, 1:2], ACT.Sqrt, bias=eps[:, :]).then_inc(g_std, 1)
                    if layer == 0:
                        act.wait_ge(g_x1T, t + 1)
                        act.activation(x1T[:, 0, :], ps_x1T[:, 0:P], ACT.Copy).then_inc(g_x1Tc, 1)
                        act.wait_ge(g_h, t + 1)
                        wait(act, g_hst, 48 * t)
                        act.activation(h_row[:, 0, :], ps_h[:, 0:HCOLS], ACT.Copy).then_inc(g_hc, 1)

                general_loop(act, step)

        @block.tensor
        def _(pe):
            pe.wait_ge(s_fill, 1)
            pe.wait_ge(s_const, 16 * 4)
            pe.transpose(ps_small[:, 0:P], w1_sb[:, :], ident[:, :])
            pe.matmul(ps_small[:, F:F + 1], w1_sb[:, :], a2_sb[:, :], start=True, stop=True).then_inc(s_w1T, 1)
            pe.wait_ge(s_lo0, 4)
            pe.wait_ge(s_w1Tc, 1)

            def group(g, g0):
                for k in range(GROUP):
                    step(g, g0, k)

            def step(g, g0, k):
                t = GROUP * g + k
                if on(t, 0):
                    wait_apart(pe, (s_trh, 2 * t + 2), (s_aggr, t - 1))
                    contract(pe, ps_agg[k % 2], edgesT[:, k % 2, :], parts0[:, :, 0:2 * F + 1], range(0, NBLK // 2), 0, NBLK - 1)
                if on(t, 1):
                    pe.wait_ge(s_aggr, t)
                    pe.wait_ge(s_xrow[(k - 1) % 4], 16 * (g + (k - 1) // 4 + 1))
                    wait(pe, s_catTc, t - 1)
                    pe.transpose(ps_catT[:, 0:P], agg[:, (k - 1) % 2, :], ident[:, :])
                    pe.transpose(ps_catT[:, P:2 * P], x_row[:, (k - 1) % 4, :], ident[:, :]).then_inc(s_catT, 1)
                if on(t, 3):
                    pe.wait_ge(s_x1, t - 2)
                    wait(pe, s_x1Tc, t - 3)
                    pe.transpose(ps_x1T[:, 0:P], x1_row[:, (k - 3) % 4, :], ident[:, :]).then_inc(s_x1T, 1)
                if on(t, 0):
                    contract(pe, ps_agg[k % 2], edgesT[:, k % 2, :], parts0[:, :, 0:2 * F + 1], range(NBLK // 2, NBLK), 0, NBLK - 1).then_inc(s_agg, 1)
                if isinstance(g, int) and g == SHIFT_GROUP and k == 1:
                    pe.wait_ge(s_max0, 1)
                    pe.transpose(ps_small[0:1, 0:P], gate[:, 0:1], ident[:, :]).then_inc(s_max0T, 1)
                if isinstance(g, int) and g == SHIFT_GROUP and k == 2:
                    pe.wait_ge(s_neg, 1)
                    pe.matmul(ps_small[:, 0:1], ones[0:1, :], verdict[0:1, 2:3], start=True, stop=True)\
                        .then_inc(s_bc, 1)
                if on(t, 1):
                    pe.wait_ge(s_catTc, t)
                    wait(pe, s_z, t - 1)
                    pe.matmul(ps_y[:, 0:F], catT[:, (k - 1) % 2, 0:P], w0_sb[:, 0, :], start=True, stop=False)
                    pe.matmul(ps_y[:, 0:F], catT[:, (k - 1) % 2, P:2 * P], w0_sb[:, 1, :],
                              start=False, stop=True).then_inc(s_y, 1)
                if on(t, 3):
                    pe.wait_ge(s_x1Tc, t - 2)
                    wait(pe, s_hc, t - 3)
                    pe.matmul(ps_h[:, 0:HCOLS], x1T[:, (k - 3) % 2, :], w1T[:, 0:HCOLS],
                              start=True, stop=True).then_inc(s_h, 1)
                if early(g, g0, k, 0):
                    bands = bands_of(g0)
                    wait_apart(pe, (s_lo1, bands), (s_partk, t - EARLY))
                    contract(pe, ps_part, edgesT[:, k % 2, :], parts1, range(0, bands * BBLK), 0, bands * BBLK - 1)\
                        .then_inc(s_part, 1)
                if making_up(g, g0, k, 0):
                    band = bands_of(g0) - 1
                    wait_apart(pe, (s_lateun, t - EARLY + 1), (s_latek, t - EARLY))
                    contract(pe, ps_small, lateT[:, k % 2, :], parts1, range(band * BBLK, (band + 1) * BBLK),
                             band * BBLK, (band + 1) * BBLK - 1, band * BBLK).then_inc(s_late, 1)

            groups_loop(pe, group, {0, SHIFT_GROUP, EARLY // GROUP})
            HEAD = NBLK - BBLK

            def head(t, first, end):
                if first == 0:
                    pe.wait_ge(s_unp, t + 1)
                return contract(pe, ps_agg[t], edgesT[:, t, :], parts1, range(first, end), 0, NBLK - 1)

            step(GROUPS, GROUPS, 0)
            pe.wait_ge(s_aggr, TILES)
            head(0, 0, HEAD // 2)
            step(GROUPS, GROUPS, 1)
            step(GROUPS, GROUPS, 2)
            head(0, HEAD // 2, HEAD).then_inc(s_head, 1)
            head(1, 0, HEAD // 2)
            pe.wait_ge(s_gate, 1)
            for c in range(3):
                last = pe.transpose(ps_small[0:1, c * P:(c + 1) * P], gate[:, c:c + 1], ident[:, :])
            last.then_inc(s_redT, 1)
            head(1, HEAD // 2, HEAD).then_inc(s_head, 1)

            pe.wait_ge(s_flag, 1)
            general = pe.value_load(flag[0:1, 0:1], min_val=0, max_val=1)
            with pe.If(general == 0):
                for t in range(2):
                    for piece in range(PIECES):
                        pe.wait_ge(s_lo1, BANDS + piece)
                        blk = range(HEAD + piece * BBLK // PIECES, HEAD + (piece + 1) * BBLK // PIECES)
                        last = contract(pe, ps_agg[t], edgesT[:, t, :], parts1, blk, 0, NBLK - 1)
                    last.then_inc(s_sum1, 1)

                def group(g, g0):
                    for k in range(GROUP):
                        t = GROUP * g + k
                        if isinstance(t, int) and t < 2:
                            continue
                        wait_apart(pe, (s_unp, t + 1), (s_sum1r, t - 1))
                        first = bands_done(g0) * BBLK
                        contract(pe, ps_agg[k % 2], edgesT[:, k % 2, :], parts1, range(first, NBLK), first, NBLK - 1)\
                            .then_inc(s_sum1, 1)

                groups_loop(pe, group, {0}, bands=bands_done)
            with pe.Else():
                pe.wait_ge(s_lo1, BANDS - 1 + PIECES)
                for t in range(2):
                    contract(pe, ps_agg[t], edgesT[:, t, :], parts1, [NBLK - 1], 0, NBLK - 1).then_inc(s_head, 1)

                def step(layer, t):
                    u = TILES * layer + t
                    pe.wait_ge(g_made, u + 1)
                    if isinstance(t, int):
                        pe.wait_ge(g_matl, 16 * (1 + 2 * layer))
                        pe.wait_ge(g_ones, 1)

                    def blocks_product(c):
                        pe.wait_ge(g_Tc, NBLK // 4 * u + c + 1)
                        for b in range(4):
                            n = 4 * c + b
                            last = pe.matmul(ps_agg[0][:, 0:HCOLS], g_blockT[:, c % 2, b * P:(b + 1) * P],
                                             g_mat[:, n, :], start=(n == 0), stop=(n == NBLK - 1))
                        last.then_inc(g_used, 1)

                    for c in range(NBLK // 4):
                        wait(pe, g_Tc, NBLK // 4 * u + c - 1)
                        for b in range(4):
                            n = 4 * c + b
                            last = pe.transpose(g_banks[c % 2][:, b * P:(b + 1) * P], g_rows[:, n * P:(n + 1) * P],
                                                ident[:, :])
                        last.then_inc(g_T, 1)
                        if c > 0:
                            blocks_product(c - 1)
                    blocks_product(NBLK // 4 - 1)
                    if layer == 0:
                        pe.wait_ge(g_agg, t + 1)
                        pe.wait_ge(g_xrow, 16 * (t + 1))
                        pe.transpose(ps_catT[:, 0:P], agg[:, 0, :], ident[:, :])
                        pe.transpose(ps_catT[:, P:2 * P], x_row[:, 0, :], ident[:, :]).then_inc(g_catT, 1)
                        pe.wait_ge(g_catTc, t + 1)
                        pe.matmul(ps_y[:, 0:F], catT[:, 0, 0:P], w0_sb[:, 0, :], start=True, stop=False)
                        pe.matmul(ps_y[:, 0:F], catT[:, 0, P:2 * P], w0_sb[:, 1, :],
                                  start=False, stop=True).then_inc(g_y, 1)
                        pe.wait_ge(g_x1, t + 1)
                        pe.transpose(ps_x1T[:, 0:P], x1_row[:, 0, :], ident[:, :]).then_inc(g_x1T, 1)
                        pe.wait_ge(g_x1Tc, t + 1)
                        pe.matmul(ps_h[:, 0:HCOLS], x1T[:, 0, :], w1T[:, 0:HCOLS], start=True, stop=True)\
                            .then_inc(g_h, 1)

                general_loop(pe, step)

        @block.vector
        def _(dve):
            dve.memset(stray[:, :], 0)
            for q in range(4):
                blk = slice(q * NBLK // 4, (q + 1) * NBLK // 4)
                dve.wait_ge(s_hi0, q + 1)
                dve.scalar_tensor_tensor(parts0[:, blk, LO:LO + F], x_stage[:, blk, :], XSCALE, parts0[:, blk, 0:F],
                                         ALU.mult, ALU.subtract).then_inc(s_lo0, 1)
            dve.wait_ge(s_const, 16 * 4)
            dve.tensor_tensor(z[:, 0, :], w1_sb[:, :], w1_sb[:, :], ALU.mult).then_inc(s_gate0, 1)
            dve.wait_ge(s_gate0, 1)
            dve.tensor_reduce(gate[:, 6:7], z[:, 0, :], AX.X, ALU.add).then_inc(s_gate0, 1)
            dve.wait_ge(s_fill, 1)
            def transpose_half(g, k, half):
                t = GROUP * g + k
                dve.wait_ge(s_conv, 2 * t + half + 1)
                wait(dve, s_agg, t - 1)
                src = edges[:, half, :, :].bitcast(u32).rearrange("p r (b w) -> p r b w", b=NB)
                dst = edgesT[:, k % 2, :].rearrange("p (b r i) -> p r b i", b=NB, r=NQ)
                dve.transpose(dst[:, 2 * half], src[:, 0])
                dve.transpose(dst[:, 2 * half + 1], src[:, 1]).then_inc(s_trh, 1)

            def exponents(s):
                dve.wait_ge(s_hload, 16 * NQ * (s + 1))
                dve.wait_ge(s_shift, 1)
                dve.tensor_scalar(h_stage(s)[:, :, F], h_stage(s)[:, :, F], shift[:, :], W_CAP, ALU.add, ALU.min)\
                    .then_inc(s_exponent, 1)

            def weighted(s, piece=0, pieces=1):
                stage = h_stage(s)[:, piece * BBLK // pieces:(piece + 1) * BBLK // pieces, :]
                dve.wait_ge(s_w, s + 1)
                dve.tensor_tensor(stage[:, :, 0:F], stage[:, :, 0:F],
                                  stage[:, :, F:F + 1].to_broadcast([P, BBLK // pieces, F]), ALU.mult)\
                    .then_inc(s_wh, 1)

            def weighted_lo(s, piece=0, pieces=1):
                dve.wait_ge(s_hi1, s + piece + 1)
                stage = h_stage(s)[:, piece * BBLK // pieces:(piece + 1) * BBLK // pieces, :]
                blk = slice(s * BBLK + piece * BBLK // pieces, s * BBLK + (piece + 1) * BBLK // pieces)
                dve.tensor_tensor(parts1[:, blk, LO:LO + F + 1], stage, parts1[:, blk, 0:F + 1],
                                  ALU.subtract).then_inc(s_lo1, 1)

            def step(g, g0, k):
                t = GROUP * g + k
                band = bands_of(g0) - 1 if k == 0 and g0 in firsts else None
                if band is not None:
                    exponents(band)
                if on(t, 0):
                    if isinstance(g, int) or bands_of(g0):
                        wait(dve, s_part, t - 1 - EARLY)
                    transpose_half(g, k, 0)
                if on(t, 1):
                    bank, s = ps_agg[(k - 1) % 2], (k - 1) % 2
                    dve.wait_ge(s_agg, t)
                    wait(dve, s_aggr, t - 1)
                    dve.reciprocal(rcount[:, :], bank[:, COUNT:COUNT + 1]).then_inc(s_rdeg, 1)
                    dve.wait_ge(s_rdeg, t)
                    dve.tensor_scalar(agg_lo[:, 0:F], bank[:, LO:LO + F], rcount[:, :], None, ALU.mult).then_inc(s_aglo, 1)
                    dve.wait_ge(s_aglo, t)
                    wait(dve, s_catT, t - 2)
                    dve.scalar_tensor_tensor(agg[:, s, :], bank[:, 0:F], rcount[:, :], agg_lo[:, 0:F],
                                             ALU.mult, ALU.add).then_inc(s_aggr, 1)
                if on(t, 2):
                    dve.wait_ge(s_y, t - 1)
                    dve.wait_ge(s_xb, t - 1)
                    wait(dve, s_x1, t - 2)
                    dve.tensor_tensor(z[:, 0, :], ps_y[:, 0:F], xb[:, k % 2, :], ALU.add).then_inc(s_z, 1)
                    dve.wait_ge(s_z, t - 1)
                    dve.bn_stats(stats[:, :], z[:, 0, :]).then_inc(s_bn, 1)
                    wait_apart(dve, (s_bn, t - 1))
                    dve.bn_aggr(mean_var[:, 0, :], stats[:, :]).then_inc(s_stats, 1)
                if making_up(g, g0, k, 0):
                    if k == 0:
                        dve.wait_ge(s_lateld, 16 * (g - EARLY // GROUP + 1))
                    wait(dve, s_late, t - 1 - EARLY)
                    dve.tensor_single_scalar(lateT[:, k % 2:k % 2 + 1, :], late_words[:, bass.ds(g % 2, 1), :],
                                             every_byte(BIT[k]), ALU.bitwise_and).then_inc(s_lateun, 1)
                if on(t, 0):
                    transpose_half(g, k, 1)
                if band is not None:
                    weighted(band)
                if early(g, g0, k, 1):
                    scale = BIT_SCALE[(k - 1) % GROUP]
                    dve.wait_ge(s_part, t - EARLY)
                    wait(dve, s_partk, t - 1 - EARLY)
                    wait(dve, s_partst[(k - 1) % 4], 16 * (g - EARLY // GROUP + (k - 1) // 4))
                    dve.tensor_scalar(part_lo[:, :], ps_part[:, LO:LO + F + 1], scale, None, ALU.mult)\
                        .then_inc(s_partlo, 1)
                    dve.wait_ge(s_partlo, t - EARLY)
                    dve.scalar_tensor_tensor(partial[:, (k - 1) % 4, :], ps_part[:, 0:F + 1], scale, part_lo[:, :],
                                             ALU.mult, ALU.add).then_inc(s_partk, 1)
                if making_up(g, g0, k, 1):
                    row = late[:, late_index(g, g0, k, 1), :]
                    dve.wait_ge(s_late, t - EARLY)
                    wait(dve, s_latek, t - 1 - EARLY)
                    dve.tensor_tensor(late_lo[:, :], ps_small[:, LO:LO + F + 1], row, ALU.add).then_inc(s_latelo, 1)
                    dve.wait_ge(s_latelo, t - EARLY)
                    dve.tensor_tensor(row, ps_small[:, 0:F + 1], late_lo[:, :], ALU.add).then_inc(s_latek, 1)
                if on(t, 0):
                    dve.wait_ge(s_trh, 2 * t + 2)
                    for part in range(CHECKS):
                        words = edgesT[:, k % 2, part * TW // CHECKS:(part + 1) * TW // CHECKS]
                        wait(dve, s_check, CHECKS * t + part)
                        dve.scalar_tensor_tensor(stray[:, :], words, every_byte(0xFF ^ EDGE[k]), stray[:, :],
                                                 ALU.bitwise_and, ALU.bitwise_or).then_inc(s_check, 1)
                    words = slice(bands_of(g0) * BW, TW)
                    bits = edgesT[:, k % 2:k % 2 + 1, words]
                    word = packed[:, bass.ds(g % 2, 1), words]
                    wait(dve, s_pack, t)
                    if k == 0:
                        wait(dve, s_pkst, 16 * (g - 1))
                        dve.tensor_single_scalar(word, bits, every_byte(BIT[k]), ALU.bitwise_and).then_inc(s_pack, 1)
                    else:
                        dve.scalar_tensor_tensor(word, bits, every_byte(BIT[k]), word, ALU.bitwise_and,
                                                 ALU.bitwise_or).then_inc(s_pack, 1)
                if on(t, 2):
                    dve.wait_ge(s_std, t - 1)
                    dve.reciprocal(rstd[:, :], std[:, 0:1]).then_inc(s_rstd, 1)
                    dve.wait_ge(s_rstd, t - 1)
                    wait(dve, s_x1st[(k - 2) % 4], 16 * (g + (k - 2) // 4))
                    dve.tensor_scalar(x1_row[:, (k - 2) % 4, :], z[:, 0, :], mean_var[:, 0, 0:1], rstd[:, :],
                                      ALU.subtract, ALU.mult).then_inc(s_x1, 1)
                if band is not None:
                    weighted_lo(band)
                if isinstance(g, int) and g == 1:
                    blk = slice(k * NBLK // GROUP, (k + 1) * NBLK // GROUP)
                    dve.tensor_reduce(x_big[:, blk], x_stage[:, blk, :], AX.X, ALU.max, apply_absolute_value=True)\
                        .then_inc(s_gate0, 1)
                if isinstance(g, int) and g == SHIFT_GROUP and k == 1:
                    dve.wait_ge(s_e, BTILES)
                    dve.tensor_reduce(gate[:, 0:1], e_all[:, 0:BTILES], AX.X, ALU.max).then_inc(s_max0, 1)
                if isinstance(g, int) and g == SHIFT_GROUP and k == 2:
                    dve.wait_ge(s_max0T, 1)
                    dve.tensor_reduce(top[0:1, 3:4], ps_small[0:1, 0:P], AX.X, ALU.max).then_inc(s_top0, 1)
                    dve.wait_ge(s_top0, 1)
                    dve.tensor_scalar(verdict[0:1, 2:3], top[0:1, 3:4], -1.0, W_SHIFT, ALU.mult, ALU.add)\
                        .then_inc(s_neg, 1)
                if isinstance(g, int) and g == SHIFT_GROUP and k == 3:
                    dve.wait_ge(s_bc, 1)
                    dve.tensor_copy(shift[:, :], ps_small[:, 0:1]).then_inc(s_shift, 1)

            def group(g, g0):
                for k in range(GROUP):
                    step(g, g0, k)

            dve.wait_ge(s_late0, 1)
            groups_loop(dve, group, {0, 1, SHIFT_GROUP, EARLY // GROUP + 1} | firsts)
            def unpack(g, m, g0, k):
                t = GROUP * g + GROUP * m + k
                words = slice(bands_done(g0) * BW, TW)
                if k == 0:
                    dve.wait_ge(s_pkld[m], 16 * (g + 2))
                wait(dve, s_sum1, t - 1)
                dve.tensor_single_scalar(edgesT[:, k % 2, words], packed_in[:, m, words], every_byte(BIT[k]),
                                         ALU.bitwise_and).then_inc(s_unp, 1)

            dve.wait_ge(s_pack, TILES)
            dve.wait_ge(s_check, CHECKS * TILES)
            unpack(0, 0, 0, 0)
            step(GROUPS, GROUPS, 0)
            dve.wait_ge(s_partk, TILES - EARLY)
            dve.wait_ge(s_latek, BANDS_LATE * BTILES)
            step(GROUPS, GROUPS, 1)
            unpack(0, 0, 0, 1)

            dve.wait_ge(s_gate0, 2 + GROUP)
            dve.tensor_reduce(gate[:, 4:5], x_big[:, :], AX.X, ALU.max)
            dve.tensor_reduce(gate[:, 5:6], x_big[:, :], AX.X, ALU.min)
            dve.tensor_reduce(gate[:, 3:4], stray[:, :].bitcast(i32), AX.X, ALU.max,
                              apply_absolute_value=True).then_inc(s_gate0, 1)
            dve.wait_ge(s_gate0, 3 + GROUP)
            dve.tensor_single_scalar(okay[:, 0:1], gate[:, 4:5], X_MAX, ALU.is_le)
            dve.tensor_single_scalar(okay[:, 1:2], gate[:, 5:6], X_MIN, ALU.is_ge)
            dve.tensor_single_scalar(okay[:, 2:3], gate[:, 6:7], W_NORM2, ALU.is_le)
            dve.tensor_single_scalar(okay[:, 3:4], gate[:, 3:4], 0.0, ALU.is_equal).then_inc(s_gate0, 1)
            dve.wait_ge(s_gate0, 4 + GROUP)
            dve.tensor_reduce(gate[:, 2:3], okay[:, :], AX.X, ALU.min, negate=True)

            dve.wait_ge(s_e, TILES)
            dve.tensor_reduce(gate[:, 0:1], e_all[:, :], AX.X, ALU.max)
            dve.tensor_reduce(gate[:, 1:2], e_all[:, :], AX.X, ALU.min, negate=True).then_inc(s_gate, 1)

            dve.wait_ge(s_redT, 1)
            dve.tensor_reduce(top[0:1, 0:3], ps_small[0:1, 0:3 * P].rearrange("o (c p) -> o c p", p=P), AX.X,
                              ALU.max).then_inc(s_top, 1)
            dve.wait_ge(s_top, 1)
            dve.tensor_scalar(verdict[0:1, 0:1], top[0:1, 0:1], top[0:1, 3:4], E_ABOVE, ALU.subtract, ALU.is_le)
            dve.tensor_scalar(verdict[0:1, 1:2], top[0:1, 1:2], top[0:1, 3:4], E_BELOW, ALU.add, ALU.is_le)\
                .then_inc(s_vord, 1)
            dve.wait_ge(s_vord, 1)
            dve.tensor_scalar(verdict[0:1, 3:4], verdict[0:1, 0:1], verdict[0:1, 1:2], top[0:1, 2:3], ALU.mult, ALU.mult)\
                .then_inc(s_vord, 1)
            dve.wait_ge(s_vord, 2)
            dve.tensor_scalar(flag[0:1, :], verdict[0:1, 3:4], 1.0, None, ALU.add).then_inc(s_flag, 1)


            exponents(BANDS - 1)
            for piece in range(PIECES):
                weighted(BANDS - 1, piece, PIECES)
            for piece in range(PIECES):
                weighted_lo(BANDS - 1, piece, PIECES)

            dve.wait_ge(s_flag, 1)
            general = dve.value_load(flag[0:1, 0:1], min_val=0, max_val=1)
            with dve.If(general == 0):
                def rows_sum(g, g0, j):
                    t, s = GROUP * g + j, j % 2
                    dve.wait_ge(s_lo1c, t + 1)
                    wait(dve, s_z1, t)
                    dve.tensor_tensor(zsum[:, :], ps_agg[s][:, 0:F + 1], agg_lo[:, 0:F + 1], ALU.add)\
                        .then_inc(s_sum1r, 1)
                    dve.wait_ge(s_sum1r, t + 1)
                    if not isinstance(g, int) or t >= LATE:
                        if isinstance(g, int) and t < EARLY:
                            done = late[:, t - LATE, :]
                        else:
                            done = part_in[:, j // GROUP % 2, j % GROUP, :]
                            if j % GROUP == 0:
                                dve.wait_ge(s_partld[j // GROUP % 2], 8 * (g - EARLY // GROUP + 2))
                        dve.tensor_tensor(zsum[:, :], zsum[:, :], done, ALU.add).then_inc(s_padd, 1)
                        dve.wait_ge(s_padd, t - LATE + 1)
                    dve.reciprocal(rcount[:, :], zsum[:, COUNT:COUNT + 1]).then_inc(s_rden, 1)
                    dve.wait_ge(s_rden, t + 1)
                    wait(dve, s_out, t - 1)
                    dve.scalar_tensor_tensor(z1[:, s, :], zsum[:, 0:F], rcount[:, :],
                                             x1_in[:, j // GROUP % 2, j % GROUP, :], ALU.mult, ALU.add).then_inc(s_z1, 1)
                    dve.wait_ge(s_z1, t + 1)
                    wait(dve, s_st1, t)
                    dve.bn_stats(stats[:, :], z1[:, s, :]).then_inc(s_bn1, 1)
                    wait_apart(dve, (s_bn1, t + 1))
                    dve.bn_aggr(mean_var[:, s, :], stats[:, :]).then_inc(s_st1, 1)

                def rows_norm(g, j):
                    t, s = GROUP * g + j, j % 2
                    dve.wait_ge(s_std1, t + 1)
                    wait(dve, s_out, t)
                    dve.reciprocal(rstd[:, :], std[:, s:s + 1]).then_inc(s_rstd1, 1)
                    dve.wait_ge(s_rstd1, t + 1)
                    wait(dve, s_outst[j % 4], 16 * (g + j // 4))
                    dve.tensor_scalar(y_out[:, j % 4, :], z1[:, s, :], mean_var[:, s, 0:1], rstd[:, :],
                                      ALU.subtract, ALU.mult).then_inc(s_out, 1)

                def pair(g, g0):
                    for j in range(2 * GROUP):
                        t = GROUP * g + j
                        if not isinstance(t, int) or t >= 2:
                            unpack(g, j // GROUP, g0, j % GROUP)
                        if on(t, 1):
                            rows_sum(g, g0, j - 1)
                        if on(t, 2):
                            rows_norm(g, j - 2)

                groups_loop(dve, pair, {0, 2, 4, EARLY // GROUP}, per=2, bands=bands_done)
                rows_sum(GROUPS, GROUPS, -1)
                rows_norm(GROUPS, -2)
                rows_norm(GROUPS, -1)

            with dve.Else():
                def step(layer, t):
                    u = TILES * layer + t
                    steps = 5 if layer == 0 else 7
                    n = [0]

                    def link(ins):
                        n[0] += 1
                        ins.then_inc(g_chain[layer], 1)
                        wait_apart(dve, (g_chain[layer], steps * t + n[0]))

                    dve.wait_ge(g_landed, 16 * (u + 1))
                    g_before(dve, layer, t)
                    if layer == 0:
                        if isinstance(t, int):
                            dve.wait_ge(s_lo1, BANDS - 1 + PIECES)
                        dve.tensor_copy(g_rows, g_adj).then_inc(g_made, 1)
                    else:
                        if isinstance(t, int):
                            dve.wait_ge(g_matl, 16 * 3)
                        link(dve.tensor_scalar(g_rows, g_adj, 0.0, -1e38, ALU.is_equal, ALU.mult))
                        link(dve.tensor_tensor(g_rows, g_rows, g_e, ALU.add))
                        link(dve.tensor_reduce(top_row[:, :], g_rows, AX.X, ALU.max))
                        dve.tensor_scalar(shift[:, :], top_row[:, :], -1.0, None, ALU.mult).then_inc(g_masked, 1)
                        dve.wait_ge(g_exp, t + 1)
                        dve.scalar_tensor_tensor(g_rows, g_adj, 0.0, g_rows, ALU.not_equal, ALU.mult)\
                            .then_inc(g_made, 1)
                    dve.wait_ge(g_used, NBLK // 4 * (u + 1))
                    dve.wait_ge(g_xrow, 16 * (u + 1))
                    link(dve.reciprocal(rcount[:, :], ps_agg[0][:, COUNT:COUNT + 1]))
                    if layer == 0:
                        dve.tensor_scalar(agg[:, 0, :], ps_agg[0][:, 0:F], rcount[:, :], None, ALU.mult).then_inc(g_agg, 1)
                        dve.wait_ge(g_y, t + 1)
                        link(dve.tensor_tensor(z[:, 0, :], ps_y[:, 0:F], bias[:, :], ALU.add))
                        link(dve.tensor_tensor(z[:, 0, :], z[:, 0, :], x_row[:, 0, :], ALU.add))
                    else:
                        link(dve.scalar_tensor_tensor(z[:, 0, :], ps_agg[0][:, 0:F], rcount[:, :], x_row[:, 0, :],
                                                      ALU.mult, ALU.add))
                    link(dve.bn_stats(stats[:, :], z[:, 0, :]))
                    dve.bn_aggr(mean_var[:, 0, :], stats[:, :]).then_inc(g_stats, 1)
                    dve.wait_ge(g_std, u + 1)
                    link(dve.reciprocal(rstd[:, :], std[:, 0:1]))
                    if layer == 0:
                        wait(dve, g_hst, 48 * t)
                        dve.tensor_scalar(x1_row[:, 0, :], z[:, 0, :], mean_var[:, 0, 0:1], rstd[:, :],
                                          ALU.subtract, ALU.mult).then_inc(g_x1, 1)
                    else:
                        wait(dve, g_outst, 16 * t)
                        dve.tensor_scalar(y_out[:, 0, :], z[:, 0, :], mean_var[:, 0, 0:1], rstd[:, :],
                                          ALU.subtract, ALU.mult).then_inc(g_out, 1)
                    assert n[0] == steps, n[0]

                general_loop(dve, step)

        @block.gpsimd
        def _(pool):
            pool.memset(ident[:, :], 0.0).then_inc(s_id, 1)
            pool.memset(ones[:, :], 1.0)
            pool.memset(eps[:, :], EPS)
            pool.memset(parts0[:, :, COUNT:COUNT + 1], XSCALE)
            pool.memset(late[:, :, :], 0.0).then_inc(s_late0, 1)
            pool.wait_ge(s_id, 1)
            pool.affine_select(out=ident[:, :], in_=ident[:, :], compare_op=ALU.not_equal, fill=1.0, base=0,
                               pattern=[[-1, P]], channel_multiplier=1).then_inc(s_fill, 1)
            pool.wait_ge(s_const, 16 * 4)

            def step(g, g0, k):
                t = GROUP * g + k
                if on(t, 4):
                    pool.wait_ge(s_hc, t - 3)
                    pool.tensor_copy(e_all[:, bass.ds(t - 4, 1)], h_row[:, k, F:F + 1]).then_inc(s_e, 1)
                if on(t, 0):
                    pool.wait_ge(s_xrow[k], 16 * (g + 1))
                    wait(pool, s_z, t - 1)
                    pool.tensor_tensor(xb[:, k % 2, :], x_row[:, k, :], bias[:, :], ALU.add).then_inc(s_xb, 1)
                if k == 0 and g0 > 0:
                    store_group(g - 1, g0 - 1)

            def store_group(g, g0):
                words = slice(bands_of(g0) * BW, TW)
                pool.wait_ge(s_pack, GROUP * (g + 1))
                wait(pool, s_pkst, 16 * g)
                pool.dma_start(packed_dram[g][:, words], packed[:, bass.ds(g % 2, 1), words].rearrange("p o w -> p (o w)"))\
                    .then_inc(s_pkst, 16)

            def group(g, g0):
                for k in range(GROUP):
                    step(g, g0, k)

            groups_loop(pool, group, {0, 1} | firsts)
            group(GROUPS, GROUPS)

            pool.wait_ge(s_flag, 1)
            general = pool.value_load(flag[0:1, 0:1], min_val=0, max_val=1)
            with pool.If(general == 0):
                pass
            with pool.Else():
                pool.wait_ge(s_lo1, BANDS - 1 + PIECES)
                pool.wait_ge(s_head, 4)
                pool.memset(g_mat[:, :, F:F + 1], 1.0).then_inc(g_ones, 1)

                def step(layer, t):
                    if layer == 0:
                        pool.wait_ge(g_hc, t + 1)
                        pool.dma_start(h_tiles[t], h_row[:, 0, :]).then_inc(g_hst, 16)
                        pool.dma_start(e_tiles[t], h_row[:, 0, F:F + 1]).then_inc(g_hst, 16)
                        pool.dma_start(x1_tiles[t], x1_row[:, 0, :]).then_inc(g_hst, 16)
                    else:
                        pool.wait_ge(g_out, t + 1)
                        pool.dma_start(out_tiles[t], y_out[:, 0, :]).then_inc(g_outst, 16)

                general_loop(pool, step)
                pool.wait_ge(g_outst, 16 * TILES)


_INS = ['x', 'adj', 'L0_gnn_weight', 'L0_gnn_bias', 'L1_gnn_W', 'L1_gnn_a']


def kernel(**inputs):
    import numpy as _np
    import concourse.bacc as _bacc
    from concourse import mybir as _mybir
    from concourse.bass_utils import run_bass_kernel_spmd as _run

    nc = _bacc.Bacc("TRN2", target_bir_lowering=False, num_devices=1)
    arrays, args = {}, []
    for name in _INS:
        a = _np.ascontiguousarray(inputs[name])
        arrays[f"in_{name}_dram"] = a
        args.append(nc.dram_tensor(f"in_{name}_dram", a.shape, _mybir.dt.from_np(a.dtype), kind="ExternalInput").ap())
    out_shape = inputs['x'].shape
    args.append(nc.dram_tensor("out_0_dram", out_shape, _mybir.dt.float32, kind="ExternalOutput").ap())
    bass_two_graph_layers(nc, *args)
    r = _run(nc, [arrays], core_ids=[0])
    return r.results[0]["out_0_dram"]
```
